# Optimizing a Trainium2 kernel written in Bass

```python
import numpy as np
import jax
import jax.numpy as jnp

def _softmax(x, axis=-1):
    return jax.nn.softmax(x, axis=axis)

def _gelu(x):
    return jax.nn.gelu(x, approximate=True)

def _silu(x):
    return jax.nn.silu(x)

def _sigmoid(x):
    return jax.nn.sigmoid(x)

def _layernorm(x, axis=-1, eps=1e-05):
    m = jnp.mean(x, axis=axis, keepdims=True)
    v = jnp.var(x, axis=axis, keepdims=True)
    return (x - m) / jnp.sqrt(v + eps)

def _scatter_add(tgt, idx, src, axis=0):
    return tgt.at[idx].add(src)

def _segment_sum(src, seg, n):
    return jax.ops.segment_sum(src, seg, n)
kernel_name = 'mk_gnn_preln_d4_gnn_r8_6a350a'

def setup_inputs(seed: int=0):
    np.random.seed(seed)
    _w = jnp.asarray

    def _rec_inputs():
        import jax
        import jax.numpy as jnp
        _gk = jax.random.key(seed)
        x = -0.000202 + 1 * jax.random.normal(jax.random.fold_in(_gk, 1), (6250, 128), jnp.float32)
        src = jax.random.randint(jax.random.fold_in(_gk, 2), (100000,), 0, 6250, jnp.int32)
        dst = jnp.minimum((6250 * jax.random.uniform(jax.random.fold_in(_gk, 3), (100000,)) ** 2.0).astype(jnp.int32), 49999)
        _o = jnp.argsort(dst, stable=True)
        src = src[_o]
        dst = dst[_o]
        return (x, src, dst)
    x, src, dst = _rec_inputs()

    def _L0_gnn_setup():
        import jax, jax.numpy as jnp
        import numpy as np
        N = 6250
        E = 100000
        D = 128
        L = 3
        BN_EPS = 1e-05

        def _bn(h, gamma, beta, mean, var):
            return (h - mean) * (gamma * jax.lax.rsqrt(var + BN_EPS)) + beta
        key = jax.random.key(seed)
        ks = jax.random.split(key, 8)
        x = jax.random.normal(ks[0], (N, D), dtype=jnp.float32)
        edge_index = jax.random.randint(ks[1], (2, E), 0, N, dtype=jnp.int32)
        s = 1.0 / np.sqrt(D)
        W1 = jax.random.uniform(ks[2], (L, D, D), jnp.float32, -s, s)
        b1 = jax.random.uniform(ks[3], (L, D), jnp.float32, -s, s)
        W2 = jax.random.uniform(ks[4], (L, D, D), jnp.float32, -s, s)
        b2 = jax.random.uniform(ks[5], (L, D), jnp.float32, -s, s)
        g = jnp.ones((L, 2, D), jnp.float32)
        be = jnp.zeros((L, 2, D), jnp.float32)
        rm = jax.random.normal(ks[6], (L, 2, D), dtype=jnp.float32) * 0.1
        rv = jax.random.uniform(ks[7], (L, 2, D), jnp.float32, 0.5, 1.5)
        return {'x': x, 'edge_index': edge_index, 'W1': W1, 'b1': b1, 'W2': W2, 'b2': b2, 'g': g, 'be': be, 'rm': rm, 'rv': rv}
    _L0_gnn_all = _L0_gnn_setup()
    _L0_gnn_in = {k: v for k, v in _L0_gnn_all.items() if k in ('W1', 'b1', 'W2', 'b2', 'g', 'be', 'rm', 'rv')}
    del _L0_gnn_all

    def _L1_gnn_setup():
        import jax, jax.numpy as jnp
        import numpy as np
        N_NODES = 6250
        N_EDGES = 100000
        DIM = 128
        BN_EPS = 1e-05
        key = jax.random.key(seed)
        ks = jax.random.split(key, 12)
        d = DIM
        s = 1.0 / np.sqrt(d)
        x = jax.random.normal(ks[0], (N_NODES, d), dtype=jnp.float32)
        edge_index = jax.random.randint(ks[1], (2, N_EDGES), 0, N_NODES, dtype=jnp.int64)
        W_msg = jax.random.uniform(ks[2], (d, d), jnp.float32, -s, s)
        b_msg = jax.random.uniform(ks[3], (d,), jnp.float32, -s, s)
        sa = 1.0 / np.sqrt(2 * d)
        W_att = jax.random.uniform(ks[4], (2 * d, 1), jnp.float32, -sa, sa)
        b_att = jax.random.uniform(ks[5], (1,), jnp.float32, -sa, sa)
        W_ih = jax.random.uniform(ks[6], (3 * d, d), jnp.float32, -s, s)
        b_ih = jax.random.uniform(ks[7], (3 * d,), jnp.float32, -s, s)
        W_hh = jax.random.uniform(ks[8], (3 * d, d), jnp.float32, -s, s)
        b_hh = jax.random.uniform(ks[9], (3 * d,), jnp.float32, -s, s)
        gamma = jnp.ones((d,), jnp.float32)
        beta = jnp.zeros((d,), jnp.float32)
        return {'x': x, 'edge_index': edge_index, 'W_msg': W_msg, 'b_msg': b_msg, 'W_att': W_att, 'b_att': b_att, 'W_ih': W_ih, 'b_ih': b_ih, 'W_hh': W_hh, 'b_hh': b_hh, 'gamma': gamma, 'beta': beta}
    _L1_gnn_all = _L1_gnn_setup()
    _L1_gnn_in = {k: v for k, v in _L1_gnn_all.items() if k in ('W_msg', 'b_msg', 'W_att', 'b_att', 'W_ih', 'b_ih', 'W_hh', 'b_hh', 'gamma', 'beta')}
    del _L1_gnn_all

    def _L2_gnn_setup():
        import jax, jax.numpy as jnp
        import numpy as np
        N, E, F, H, L = (6250, 75000, 128, 128, 5)
        key = jax.random.key(seed)
        ks = jax.random.split(key, 16)
        s = 1.0 / np.sqrt(H)
        u = lambda k, shape: jax.random.uniform(k, shape, jnp.float32, -s, s)
        return {'x': jax.random.normal(ks[0], (N, F), jnp.float32), 'edge_index': jax.random.randint(ks[1], (2, E), 0, N, jnp.int64), 'enc_w1': u(ks[2], (H, F)), 'enc_b1': u(ks[3], (H,)), 'enc_w2': u(ks[4], (H, H)), 'enc_b2': u(ks[5], (H,)), 'conv_w': u(ks[6], (L, H, H)), 'gru_wih': u(ks[7], (3 * H, H)), 'gru_whh': u(ks[8], (3 * H, H)), 'gru_bih': u(ks[9], (3 * H,)), 'gru_bhh': u(ks[10], (3 * H,)), 'dec_w1': u(ks[11], (H, H)), 'dec_b1': u(ks[12], (H,)), 'dec_w2': u(ks[13], (F, H)), 'dec_b2': u(ks[14], (F,))}
    _L2_gnn_all = _L2_gnn_setup()
    _L2_gnn_in = {k: v for k, v in _L2_gnn_all.items() if k in ('enc_w1', 'enc_b1', 'enc_w2', 'enc_b2', 'conv_w', 'gru_wih', 'gru_whh', 'gru_bih', 'gru_bhh', 'dec_w1', 'dec_b1', 'dec_w2', 'dec_b2')}
    del _L2_gnn_all

    def _L3_gnn_setup():
        import jax, jax.numpy as jnp
        import numpy as np
        N_NODES = 6250
        N_EDGES = 100000
        D_IN = 128
        D_OUT = 128
        key = jax.random.key(seed)
        k1, k2, k3, k4 = jax.random.split(key, 4)
        node_features = jax.random.normal(k1, (N_NODES, D_IN), dtype=jnp.float32)
        edge_index = jax.random.randint(k2, (2, N_EDGES), 0, N_NODES, dtype=jnp.int64)
        W = jax.random.normal(k3, (D_OUT, D_IN), dtype=jnp.float32) / np.sqrt(D_IN)
        b = jax.random.normal(k4, (D_OUT,), dtype=jnp.float32) * 0.01
        return {'node_features': node_features, 'edge_index': edge_index, 'W': W, 'b': b}
    _L3_gnn_all = _L3_gnn_setup()
    _L3_gnn_in = {k: v for k, v in _L3_gnn_all.items() if k in ('W', 'b')}
    del _L3_gnn_all
    return {'x': x, 'src': src, 'dst': dst, 'L0_gnn_W1': _L0_gnn_in['W1'], 'L0_gnn_b1': _L0_gnn_in['b1'], 'L0_gnn_W2': _L0_gnn_in['W2'], 'L0_gnn_b2': _L0_gnn_in['b2'], 'L0_gnn_g': _L0_gnn_in['g'], 'L0_gnn_be': _L0_gnn_in['be'], 'L0_gnn_rm': _L0_gnn_in['rm'], 'L0_gnn_rv': _L0_gnn_in['rv'], 'L1_gnn_W_msg': _L1_gnn_in['W_msg'], 'L1_gnn_b_msg': _L1_gnn_in['b_msg'], 'L1_gnn_W_att': _L1_gnn_in['W_att'], 'L1_gnn_b_att': _L1_gnn_in['b_att'], 'L1_gnn_W_ih': _L1_gnn_in['W_ih'], 'L1_gnn_b_ih': _L1_gnn_in['b_ih'], 'L1_gnn_W_hh': _L1_gnn_in['W_hh'], 'L1_gnn_b_hh': _L1_gnn_in['b_hh'], 'L1_gnn_gamma': _L1_gnn_in['gamma'], 'L1_gnn_beta': _L1_gnn_in['beta'], 'L2_gnn_enc_w1': _L2_gnn_in['enc_w1'], 'L2_gnn_enc_b1': _L2_gnn_in['enc_b1'], 'L2_gnn_enc_w2': _L2_gnn_in['enc_w2'], 'L2_gnn_enc_b2': _L2_gnn_in['enc_b2'], 'L2_gnn_conv_w': _L2_gnn_in['conv_w'], 'L2_gnn_gru_wih': _L2_gnn_in['gru_wih'], 'L2_gnn_gru_whh': _L2_gnn_in['gru_whh'], 'L2_gnn_gru_bih': _L2_gnn_in['gru_bih'], 'L2_gnn_gru_bhh': _L2_gnn_in['gru_bhh'], 'L2_gnn_dec_w1': _L2_gnn_in['dec_w1'], 'L2_gnn_dec_b1': _L2_gnn_in['dec_b1'], 'L2_gnn_dec_w2': _L2_gnn_in['dec_w2'], 'L2_gnn_dec_b2': _L2_gnn_in['dec_b2'], 'L3_gnn_W': _L3_gnn_in['W'], 'L3_gnn_b': _L3_gnn_in['b']}

def reference(x, src, dst, L0_gnn_W1, L0_gnn_b1, L0_gnn_W2, L0_gnn_b2, L0_gnn_g, L0_gnn_be, L0_gnn_rm, L0_gnn_rv, L1_gnn_W_msg, L1_gnn_b_msg, L1_gnn_W_att, L1_gnn_b_att, L1_gnn_W_ih, L1_gnn_b_ih, L1_gnn_W_hh, L1_gnn_b_hh, L1_gnn_gamma, L1_gnn_beta, L2_gnn_enc_w1, L2_gnn_enc_b1, L2_gnn_enc_w2, L2_gnn_enc_b2, L2_gnn_conv_w, L2_gnn_gru_wih, L2_gnn_gru_whh, L2_gnn_gru_bih, L2_gnn_gru_bhh, L2_gnn_dec_w1, L2_gnn_dec_b1, L2_gnn_dec_w2, L2_gnn_dec_b2, L3_gnn_W, L3_gnn_b):
    import jax
    import jax.numpy as jnp

    def _L0_gnn_ref(x, edge_index, W1, b1, W2, b2, g, be, rm, rv):
        import jax, jax.numpy as jnp
        import numpy as np
        N = 6250
        E = 100000
        D = 128
        L = 3
        BN_EPS = 1e-05

        def _bn(h, gamma, beta, mean, var):
            return (h - mean) * (gamma * jax.lax.rsqrt(var + BN_EPS)) + beta
        src, dst = (edge_index[0], edge_index[1])
        h = x
        for i in range(L):
            agg = jax.ops.segment_sum(h[src], dst, num_segments=N)
            h = h + agg
            h = jnp.maximum(_bn(h @ W1[i] + b1[i], g[i, 0], be[i, 0], rm[i, 0], rv[i, 0]), 0.0)
            h = h @ W2[i] + b2[i]
            h = jnp.maximum(_bn(h, g[i, 1], be[i, 1], rm[i, 1], rv[i, 1]), 0.0)
        return h

    def _L1_gnn_ref(x, edge_index, W_msg, b_msg, W_att, b_att, W_ih, b_ih, W_hh, b_hh, gamma, beta):
        import jax, jax.numpy as jnp
        import numpy as np
        N_NODES = 6250
        N_EDGES = 100000
        DIM = 128
        BN_EPS = 1e-05
        num_nodes, d = x.shape
        src = edge_index[0]
        dst = edge_index[1]
        xs = x[src]
        xd = x[dst]
        att = jax.nn.sigmoid(xs @ W_att[:d] + xd @ W_att[d:] + b_att)
        messages = (xs @ W_msg + b_msg) * att
        aggregated = jax.ops.segment_sum(messages, dst, num_segments=num_nodes)
        gi = aggregated @ W_ih.T + b_ih
        gh = x @ W_hh.T + b_hh
        i_r, i_z, i_n = jnp.split(gi, 3, axis=1)
        h_r, h_z, h_n = jnp.split(gh, 3, axis=1)
        r = jax.nn.sigmoid(i_r + h_r)
        z = jax.nn.sigmoid(i_z + h_z)
        n = jnp.tanh(i_n + r * h_n)
        h_new = (1.0 - z) * n + z * x
        mean = jnp.mean(h_new, axis=0)
        var = jnp.var(h_new, axis=0)
        return gamma * (h_new - mean) * jax.lax.rsqrt(var + BN_EPS) + beta

    def _L2_gnn_ref(x, edge_index, enc_w1, enc_b1, enc_w2, enc_b2, conv_w, gru_wih, gru_whh, gru_bih, gru_bhh, dec_w1, dec_b1, dec_w2, dec_b2):
        import jax, jax.numpy as jnp
        import numpy as np
        N, E, F, H, L = (6250, 75000, 128, 128, 5)
        src, dst = (edge_index[0], edge_index[1])
        n_nodes = x.shape[0]
        h = jnp.maximum(x @ enc_w1.T + enc_b1, 0.0) @ enc_w2.T + enc_b2

        def step(h, w):
            m = h @ w
            agg = jax.ops.segment_sum(m[src], dst, num_segments=n_nodes)
            gi = agg @ gru_wih.T + gru_bih
            gh = h @ gru_whh.T + gru_bhh
            ir, iz, i_n = jnp.split(gi, 3, axis=1)
            hr, hz, h_n = jnp.split(gh, 3, axis=1)
            r = jax.nn.sigmoid(ir + hr)
            z = jax.nn.sigmoid(iz + hz)
            n = jnp.tanh(i_n + r * h_n)
            return ((1.0 - z) * n + z * h, None)
        h, _ = jax.lax.scan(step, h, conv_w)
        h = jnp.maximum(h, 0.0)
        out = jnp.maximum(h @ dec_w1.T + dec_b1, 0.0) @ dec_w2.T + dec_b2
        return jax.nn.sigmoid(out)

    def _L3_gnn_ref(node_features, edge_index, W, b):
        import jax, jax.numpy as jnp
        import numpy as np
        N_NODES = 6250
        N_EDGES = 100000
        D_IN = 128
        D_OUT = 128
        source_nodes = edge_index[0]
        dest_nodes = edge_index[1]
        neighbor_features = node_features[source_nodes]
        aggregated = jax.ops.segment_sum(neighbor_features, dest_nodes, num_segments=node_features.shape[0])
        return aggregated @ W.T + b
    edge_index = jnp.stack([src, dst])
    h = jnp.maximum(_layernorm(x, axis=-1), 0.0)
    x = x + _L0_gnn_ref(h, edge_index, L0_gnn_W1, L0_gnn_b1, L0_gnn_W2, L0_gnn_b2, L0_gnn_g, L0_gnn_be, L0_gnn_rm, L0_gnn_rv)
    h = jnp.maximum(_layernorm(x, axis=-1), 0.0)
    x = x + _L1_gnn_ref(h, edge_index, L1_gnn_W_msg, L1_gnn_b_msg, L1_gnn_W_att, L1_gnn_b_att, L1_gnn_W_ih, L1_gnn_b_ih, L1_gnn_W_hh, L1_gnn_b_hh, L1_gnn_gamma, L1_gnn_beta)
    h = jnp.maximum(_layernorm(x, axis=-1), 0.0)
    x = x + _L2_gnn_ref(h, edge_index, L2_gnn_enc_w1, L2_gnn_enc_b1, L2_gnn_enc_w2, L2_gnn_enc_b2, L2_gnn_conv_w, L2_gnn_gru_wih, L2_gnn_gru_whh, L2_gnn_gru_bih, L2_gnn_gru_bhh, L2_gnn_dec_w1, L2_gnn_dec_b1, L2_gnn_dec_w2, L2_gnn_dec_b2)
    h = jnp.maximum(_layernorm(x, axis=-1), 0.0)
    x = x + _L3_gnn_ref(h, edge_index, L3_gnn_W, L3_gnn_b)
    return x

_drawn_inputs = setup_inputs


def setup_inputs(seed=0):
    import zlib

    import numpy as np

    out = dict(_drawn_inputs(seed))
    spreads = {'L0_gnn_g': (1.0, 0.2),
     'L0_gnn_be': (0.0, 0.1),
     'L1_gnn_gamma': (1.0, 0.6),
     'L1_gnn_beta': (0.0, 0.8)}
    factors = {'L0_gnn_b1': 5.004,
     'L1_gnn_b_msg': 5.509,
     'L1_gnn_W_att': 28.048,
     'L1_gnn_b_ih': 27.179,
     'L1_gnn_W_hh': 4.71,
     'L1_gnn_b_hh': 58.421,
     'L2_gnn_enc_w1': 107.101,
     'L2_gnn_enc_b1': 106.507,
     'L2_gnn_enc_w2': 29.574,
     'L2_gnn_enc_b2': 200.0,
     'L2_gnn_conv_w': 100.074,
     'L2_gnn_gru_wih': 77.832,
     'L2_gnn_gru_whh': 200.0,
     'L2_gnn_gru_bih': 200.0,
     'L2_gnn_gru_bhh': 200.0,
     'L2_gnn_dec_w1': 29.646,
     'L2_gnn_dec_b1': 200.0,
     'L2_gnn_dec_w2': 8.0,
     'L2_gnn_dec_b2': 200.0,
     'L3_gnn_b': 199.904}
    for name, (base, spread) in spreads.items():
        noise = np.random.default_rng([zlib.crc32(name.encode()), seed]).standard_normal(out[name].shape)
        drawn = base * np.exp(spread * noise) if base else spread * noise
        out[name] = jnp.asarray(drawn.astype(out[name].dtype))
    for name, factor in factors.items():
        out[name] = (out[name] * factor).astype(out[name].dtype)
    return out
```

```python
from contextlib import ExitStack, contextmanager

import numpy as np

import concourse.bass as bass
from concourse import mybir

F32 = mybir.dt.float32
BF16 = mybir.dt.bfloat16
I32 = mybir.dt.int32
U32 = mybir.dt.uint32
ALU = mybir.AluOpType
ACT = mybir.ActivationFunctionType

N = 6250
E = 100000
D = 128
P = 128
NB = -(-N // P)
NP = NB * P
SLAB_BLOCKS = 7
NSLAB = NB // SLAB_BLOCKS
SLAB = SLAB_BLOCKS * P
CW = 448
NCH = NP // CW
HC = NCH // 2
HALF = HC * CW
SLOTS = 7
LN_EPS = 1e-5
assert NB % SLAB_BLOCKS == 0 and NP % CW == 0 and NCH % 2 == 0 and SLAB == 2 * CW and NB % SLOTS == 0

PARTS = [(0, 4), (4, 3)]

SRC_SHIFT = 13
PITCH = 1 << SRC_SHIFT
KEY_BASE = 0x20000000
KEY_MASK = KEY_BASE - 1
GROUP = 4
TROWS = 112
TCH = 7
NT = TROWS * TCH
NG = NT // GROUP
GW = GROUP * P
FULL_T, TAIL = divmod(E, P)
assert NT * P >= E and NP <= PITCH and NG % 4 == 0
FIRST_MARK = 1024
PAD_TARGET = 1024


class Semaphores(dict):
    credited = frozenset()


@contextmanager
def stage(nc, *names, credited=()):
    s = Semaphores((n, nc.alloc_semaphore(f"{n}_{nc.next_id()}")) for n in (*names, *credited))
    s.credited = frozenset(credited)
    for name in credited:
        nc.gpsimd.sem_inc(s[name])
    if credited:
        nc.all_engine_barrier()
    with nc.Block() as block:
        yield block, s
    nc.clear_and_free_semaphores(list(s.values()))
    nc.all_engine_barrier()


def pairs(*names):
    return [f"{n}{u}" for n in names for u in (0, 1)]


def wait(engine, s, name, value):
    engine.wait_ge(s[name], value + (name in s.credited))
    if not isinstance(value, int):
        engine.sem_inc(s["passed"])


def scratch(nc, ctx, name, shape, dt=F32):
    return ctx.enter_context(nc.sbuf_tensor(f"{name}_{nc.next_id()}", shape, dt))


class Chain:

    def __init__(self, engine, sem):
        self.engine, self.sem, self.n = engine, sem, 0

    def add(self, instruction):
        instruction.then_inc(self.sem, 1)
        self.n += 1
        return instruction

    def sync(self):
        self.engine.wait_ge(self.sem, self.n)

    def restart(self):
        self.sync()
        self.engine.sem_clear(self.sem)
        self.n = 0


def build_counts(nc, src, dst, count):
    keyrow = nc.dram_tensor("keyrow", [NT * P], F32, kind="Internal").ap()
    with ExitStack() as ctx:
        def sb(name, shape, dt):
            return ctx.enter_context(nc.sbuf_tensor(name, shape, dt))

        ident = sb("b_ident", [P, P], F32)
        s_rows = sb("s_rows", [TROWS, TCH, P], I32)
        d_rows = sb("d_rows", [TROWS, TCH, P], I32)
        key_rows = sb("key_rows", [TROWS, TCH, P], I32)
        keyT = sb("keyT", [P, NT], F32)
        zeros = sb("zeros", [P, NP], BF16)
        order_i = sb("order_i", [P, GROUP, GW], I32)
        weight = sb("weight", [P, GROUP, GW], F32)
        dump_i = sb("dump_i", [P, GROUP], I32)
        dump = sb("dump", [P, GROUP], I32)
        rows = [sb(f"rows{b}", [P, 2 * GW], F32) for b in (0, 1)]
        junk = sb("junk", [P, GROUP, GW], BF16)
        acc = sb("acc", [P, GROUP], F32)
        repeated = sb("repeated", [P, GROUP], U32)
        where = sb("where", [P, GROUP], I32)
        index = [sb(f"index{b}", [P, GROUP], U32) for b in (0, 1)]
        amount = [sb(f"amount{b}", [P, GROUP], BF16) for b in (0, 1)]
        ps = ctx.enter_context(nc.psum_tensor("b_ps", [P, 2, 512], F32))

        with stage(nc, "pad", "edges", "id0", "id1", "ord", "dve", "keys", "tr", "kout") as (block, s):
            whole = (TCH - 1) * TROWS

            @block.gpsimd
            def _(e):
                e.memset(ident[:, :], 0.0).then_inc(s["id0"], 1)
                wait(e, s, "id0", 1)
                e.affine_select(out=ident[:, :], in_=ident[:, :], compare_op=ALU.not_equal, fill=1.0, base=0,
                                pattern=[[-1, P]], channel_multiplier=1).then_inc(s["id1"], 1)
                e.iota(order_i[:, :, :], pattern=[[P, GROUP], [-1, GW]], base=0, channel_multiplier=1)\
                    .then_inc(s["ord"], 1)
                e.iota(dump_i[:, :], pattern=[[P, GROUP]], base=NP << SRC_SHIFT, channel_multiplier=1)\
                    .then_inc(s["ord"], 1)

            @block.sync
            def _(e):
                for n, (edges, tile) in enumerate(((src, s_rows), (dst, d_rows))):
                    e.dma_start(tile[:, 0:TCH - 1, :], edges[0:whole * P].rearrange("(c p l) -> p c l", p=TROWS, l=P))\
                        .then_inc(s["edges"], 16)
                    wait(e, s, "pad", 2 * n + 2)
                    e.dma_start(tile[0:FULL_T - whole, TCH - 1, :],
                                edges[whole * P:FULL_T * P].rearrange("(p l) -> p l", l=P)).then_inc(s["edges"], 16)
                    e.dma_start(tile[FULL_T - whole:FULL_T - whole + 1, TCH - 1, 0:TAIL],
                                edges[FULL_T * P:E].rearrange("(a l) -> a l", a=1)).then_inc(s["edges"], 16)
                wait(e, s, "keys", 1)
                e.dma_start(keyrow.rearrange("(c p l) -> p c l", p=TROWS, l=P), key_rows[:, :, :].bitcast(F32))\
                    .then_inc(s["kout"], 16)
                wait(e, s, "kout", 16)

            @block.vector
            def _(e):
                ch = Chain(e, s["dve"])
                for tile, value in ((s_rows, NP), (d_rows, PAD_TARGET)):
                    e.memset(tile[:, TCH - 1, :], value).then_inc(s["pad"], 2)
                ch.add(e.memset(zeros[:, :], 0.0))
                wait(e, s, "ord", 2)
                ch.add(e.tensor_scalar(weight[:, :, :], order_i[:, :, :], 0.0, float(FIRST_MARK), ALU.is_gt, ALU.mult))
                ch.add(e.tensor_scalar(dump[:, :], dump_i[:, :], KEY_BASE, None, ALU.bitwise_or))
                ch.sync()
                ch.add(e.tensor_scalar(weight[:, :, :], weight[:, :, :], 1.0, None, ALU.add))
                wait(e, s, "edges", 6 * 16)
                ch.add(e.tensor_scalar(key_rows[:, :, :], s_rows[:, :, :], SRC_SHIFT, KEY_BASE,
                                       ALU.logical_shift_left, ALU.bitwise_or))
                ch.sync()
                e.tensor_tensor(key_rows[:, :, :], key_rows[:, :, :], d_rows[:, :, :], ALU.bitwise_or)\
                    .then_inc(s["keys"], 1)
                for c in range(TCH):
                    wait(e, s, "tr", c + 1)
                    ch.add(e.tensor_copy(keyT[:, c * TROWS:(c + 1) * TROWS], ps[:, c % 2, 0:TROWS]))
                ch.sync()

            @block.tensor
            def _(e):
                wait(e, s, "keys", 1)
                wait(e, s, "id1", 1)
                for c in range(TCH):
                    if c >= 2:
                        wait(e, s, "dve", 5 + c - 1)
                    e.transpose(ps[:, c % 2, 0:TROWS], key_rows[:, c, :].bitcast(F32), ident[0:TROWS, 0:TROWS])\
                        .then_inc(s["tr"], 1)

        table = count.rearrange("(s t) o -> s (t o)", t=PITCH)
        with stage(nc, "zero", "dve", "landed", "passed", *pairs("load", "made"), credited=pairs("used", "freed")) as (block, s):
            @block.sync
            def _(e):
                e.dma_start(table[NP:NP + 1, :].rearrange("a (p t) -> (a p) t", p=16), zeros[0:16, 0:PITCH // 16])\
                    .then_inc(s["zero"], 16)
                with e.Fori(0, NB) as k:
                    e.dma_start(table[bass.ds(k * P, P), 0:NP], zeros[:, :]).then_inc(s["zero"], 16)
                with e.Fori(0, NG // 4) as i:
                    for b in (0, 1):
                        wait(e, s, f"used{b}", i)
                        e.dma_start(rows[b][:, :], keyrow[bass.ds(i * (4 * GW) + b * 2 * GW, 2 * GW)]
                                    .rearrange("(a l) -> a l", a=1).to_broadcast([P, 2 * GW]))\
                            .then_inc(s[f"load{b}"], 16)
                wait(e, s, "used0", NG // 4)
                wait(e, s, "used1", NG // 4)

            @block.vector
            def _(e):
                ch = Chain(e, s["dve"])
                with e.Fori(0, NG // 4) as i:
                    for g in range(4):
                        b, o = g // 2, g % 2
                        if o == 0:
                            wait(e, s, f"load{b}", i * 16 + 16)
                        col = i * (4 * GROUP) + g * GROUP
                        ch.sync()
                        for t in range(GROUP):
                            ins = ch.add(e.scalar_tensor_tensor(
                                junk[:, t, :], rows[b][:, o * GW:(o + 1) * GW], keyT[:, bass.ds(col + t, 1)],
                                weight[:, t, :], ALU.is_equal, ALU.mult, accum_out=acc[:, t:t + 1]))
                        ch.add(e.tensor_copy(where[:, :], keyT[:, bass.ds(col, GROUP)].bitcast(I32)))
                        ch.sync()
                        if o == 1:
                            e.sem_inc(s[f"used{b}"])
                        ch.add(e.tensor_scalar(repeated[:, :], acc[:, :], FIRST_MARK - 0.5, None, ALU.is_gt))
                        ch.sync()
                        ch.add(e.copy_predicated(where[:, :], repeated[:, :], dump[:, :]))
                        ch.sync()
                        wait(e, s, f"freed{o}", i * 2 + b)
                        ch.add(e.scalar_tensor_tensor(amount[o][:, :], acc[:, :], FIRST_MARK - 0.5, acc[:, :],
                                                      ALU.is_lt, ALU.mult))
                        ch.add(e.tensor_scalar(index[o][:, :], where[:, :].bitcast(U32), KEY_MASK, None, ALU.bitwise_and))
                        ch.sync()
                        e.sem_inc(s[f"made{o}"])
                    ch.restart()

            @block.gpsimd
            def _(e):
                wait(e, s, "zero", 16 * (NB + 1))
                with e.Fori(0, NG // 4) as i:
                    for g in range(4):
                        b, o = g // 2, g % 2
                        wait(e, s, f"made{o}", i * 2 + b + 1)
                        for t in range(GROUP):
                            e.indirect_dma_start(
                                out=count, out_offset=bass.IndirectOffsetOnAxis(ap=index[o][:, t:t + 1], axis=0),
                                in_=amount[o][:, t:t + 1], in_offset=None, compute_op=ALU.add)\
                                .then_inc(s["landed"], 16)
                        wait(e, s, "landed", i * (4 * GROUP * 16) + (g + 1) * GROUP * 16)
                        e.sem_inc(s[f"freed{o}"])


class Net:

    def __init__(self, nc, ctx, count):
        self.nc, self.ctx, self.count = nc, ctx, count
        sb = self.sb
        self.hT = sb("hT", [P, NP])
        self.aggT = sb("aggT", [P, NP])
        self.xN = sb("xN", [P, NP])
        self.h3 = sb("h3", [P, 3, NP], BF16)
        self.msg = sb("msg", [P, NP])
        self.ring = sb("ring", [P, SLOTS, HALF], BF16)
        self.ident = sb("ident", [P, P])
        self.zero = sb("zero", [P, CW], BF16)
        self.eps = sb("eps", [P, 1])
        self.part = [sb(f"part{u}", [P, nb * P]) for u, (_, nb) in enumerate(PARTS)]
        self.rest = [sb(f"rest{u}", [P, nb * P]) for u, (_, nb) in enumerate(PARTS)]
        self.ps = ctx.enter_context(nc.psum_tensor("ps", [P, 8, 512], F32))

    def sb(self, name, shape, dt=F32):
        return self.ctx.enter_context(self.nc.sbuf_tensor(name, shape, dt))

    def room(self, n):
        return self.h3[:, :, :].rearrange("p a t -> p (a t)").bitcast(F32)[:, n * CW:(n + 1) * CW]


    def setup(self, x, matrices, vectors, directs):
        nc, P_ = self.nc, P
        full = (N // P) * P
        nm = len(matrices)
        self.wT = self.sb("wT", [P, nm, P])
        with ExitStack() as tmp:
            raw = self.ring[:, 0:3, :].rearrange("p s t -> p (s t)").bitcast(F32)[:, 0:nm * P]\
                .rearrange("p (m t) -> p m t", t=P)
            with stage(nc, "id0", "cst", "x0", "x1", "w", "v", "tr", "cp") as (block, s):
                @block.gpsimd
                def _(e):
                    e.memset(self.ident[:, :], 0.0).then_inc(s["id0"], 1)
                    wait(e, s, "id0", 1)
                    e.affine_select(out=self.ident[:, :], in_=self.ident[:, :], compare_op=ALU.not_equal, fill=1.0,
                                    base=0, pattern=[[-1, P]], channel_multiplier=1).then_inc(s["cst"], 1)
                    e.memset(self.zero[:, :], 0.0).then_inc(s["cst"], 1)
                    e.memset(self.eps[:, :], LN_EPS).then_inc(s["cst"], 1)
                    wait(e, s, "cst", 3)

                @block.sync
                def _(e):
                    e.dma_start(self.xN[:, 0:full].rearrange("p (k f) -> p k f", f=D),
                                x[0:full, :].rearrange("(k p) f -> p k f", p=P)).then_inc(s["x1"], 16)
                    for i, m in enumerate(matrices):
                        e.dma_start(raw[:, i, :], m).then_inc(s["w"], 16)
                    wait(e, s, "x0", 1)
                    e.dma_start(self.xN[0:N - full, full:NP], x[full:N, :]).then_inc(s["x1"], 16)
                    with nc.allow_non_contiguous_dma(reason="vectors of 128 words, one to a partition"):
                        for tile, v in vectors:
                            e.dma_start(tile, v).then_inc(s["v"], 16)
                    for tile, v in directs:
                        e.dma_start(tile, v).then_inc(s["v"], 16)
                    wait(e, s, "x1", 32)
                    wait(e, s, "v", 16 * (len(vectors) + len(directs)))

                @block.vector
                def _(e):
                    e.memset(self.xN[:, full:NP], 0.0).then_inc(s["x0"], 1)
                    for i in range(nm):
                        wait(e, s, "tr", i + 1)
                        e.tensor_copy(self.wT[:, i, :], self.ps[:, i % 8, 0:P]).then_inc(s["cp"], 1)
                    wait(e, s, "cp", nm)

                @block.tensor
                def _(e):
                    wait(e, s, "cst", 3)
                    wait(e, s, "w", 16 * nm)
                    for i in range(nm):
                        if i >= 8:
                            wait(e, s, "cp", i - 7)
                        e.transpose(self.ps[:, i % 8, 0:P], raw[:, i, :], self.ident[:, :]).then_inc(s["tr"], 1)

    @staticmethod
    def rsqrt(ch, y, var, root, t):
        e = ch.engine
        ch.add(e.reciprocal(y, root)); ch.sync()
        ch.add(e.tensor_tensor(t, y, y, ALU.mult)); ch.sync()
        ch.add(e.scalar_tensor_tensor(t, var, LN_EPS, t, ALU.add, ALU.mult)); ch.sync()
        ch.add(e.tensor_scalar(t, t, -0.5, 1.5, ALU.mult, ALU.add)); ch.sync()
        ch.add(e.tensor_tensor(y, y, t, ALU.mult)); ch.sync()


    def norm(self, add, to_hT, to_parts):
        nc, ps = self.nc, self.ps
        names = ["passed", "dve", "act"] + pairs("cut", "stats", "root", "inv", "normed", "hi", "rest", "mid")
        credited = pairs(*["turned", "added"] * add, *["turned_h", "stored"] * to_hT)
        with ExitStack() as tmp, stage(nc, *names, credited=credited) as (block, s):
            def sb(n, shape):
                return scratch(nc, tmp, n, shape)
            stats = [sb(f"stats{u}", [P, nb, 6]) for u, (_, nb) in enumerate(PARTS)]
            mv = [sb(f"mv{u}", [P, nb, 2]) for u, (_, nb) in enumerate(PARTS)]
            root = [sb(f"root{u}", [P, nb]) for u, (_, nb) in enumerate(PARTS)]
            inv = [sb(f"inv{u}", [P, nb]) for u, (_, nb) in enumerate(PARTS)]
            off = [sb(f"off{u}", [P, nb]) for u, (_, nb) in enumerate(PARTS)]
            tmp1 = [sb(f"tmp1{u}", [P, nb]) for u, (_, nb) in enumerate(PARTS)]
            hN = [sb(f"hN{u}", [P, nb * P]) for u, (_, nb) in enumerate(PARTS)]

            def cols(i, u):
                b0, nb = PARTS[u]
                return bass.ds(i * SLAB + b0 * P, nb * P)

            if add:
                @block.gpsimd
                def _(e):
                    with e.Fori(0, NSLAB) as i:
                        for u in (0, 1):
                            wait(e, s, f"turned{u}", i)
                            e.tensor_copy(self.part[u][:, :], self.hT[:, cols(i, u)]).then_inc(s[f"cut{u}"], 1)

            @block.tensor
            def _(e):
                with e.Fori(0, NSLAB) as i:
                    for u, (_, nb) in enumerate(PARTS):
                        if add:
                            wait(e, s, f"cut{u}", i + 1)
                            wait(e, s, f"added{u}", i)
                            for b in range(nb):
                                ins = e.transpose(ps[:, u, b * P:(b + 1) * P], self.part[u][:, b * P:(b + 1) * P],
                                                  self.ident[:, :])
                            ins.then_inc(s[f"turned{u}"], 1)
                    for u, (_, nb) in enumerate(PARTS):
                        if to_hT:
                            wait(e, s, f"normed{u}", i + 1)
                            wait(e, s, f"stored{u}", i)
                            for b in range(nb):
                                ins = e.transpose(ps[:, 2 + u, b * P:(b + 1) * P], hN[u][:, b * P:(b + 1) * P],
                                                  self.ident[:, :])
                            ins.then_inc(s[f"turned_h{u}"], 1)

            @block.vector
            def _(e):
                ch = Chain(e, s["dve"])
                with e.Fori(0, NSLAB) as i:
                    for u, (b0, nb) in enumerate(PARTS):
                        if add:
                            wait(e, s, f"turned{u}", i + 1)
                            ch.add(e.tensor_tensor(self.xN[:, cols(i, u)], ps[:, u, 0:nb * P], self.xN[:, cols(i, u)],
                                                   ALU.add))
                            ch.sync()
                            e.sem_inc(s[f"added{u}"])
                        for b in range(nb):
                            ch.add(e.bn_stats(stats[u][:, b, :], self.xN[:, bass.ds(i * SLAB + (b0 + b) * P, P)]))
                        ch.sync()
                        for b in range(nb):
                            ch.add(e.bn_aggr(mv[u][:, b, :], stats[u][:, b, :]))
                        ch.sync()
                        e.sem_inc(s[f"stats{u}"])
                    for u, (b0, nb) in enumerate(PARTS):
                        wait(e, s, f"root{u}", i + 1)
                        self.rsqrt(ch, inv[u][:, :], mv[u][:, :, 1], root[u][:, :], tmp1[u][:, :])
                        ch.add(e.scalar_tensor_tensor(off[u][:, :], mv[u][:, :, 0], -1.0, inv[u][:, :],
                                                      ALU.mult, ALU.mult))
                        ch.sync()
                        e.sem_inc(s[f"inv{u}"])
                    for u, (b0, nb) in enumerate(PARTS):
                        if to_hT:
                            wait(e, s, f"turned_h{u}", i + 1)
                            ch.add(e.tensor_copy(self.hT[:, cols(i, u)], ps[:, 2 + u, 0:nb * P]))
                            ch.sync()
                            e.sem_inc(s[f"stored{u}"])
                        if to_parts:
                            wait(e, s, f"hi{u}", i + 1)
                            ch.add(e.tensor_tensor(self.rest[u][:, :], hN[u][:, :], self.h3[:, 0, cols(i, u)], ALU.subtract))
                            ch.sync()
                            e.sem_inc(s[f"rest{u}"])
                    for u, (b0, nb) in enumerate(PARTS):
                        if to_parts:
                            wait(e, s, f"mid{u}", i + 1)
                            ch.add(e.tensor_tensor(self.h3[:, 2, cols(i, u)], self.rest[u][:, :], self.h3[:, 1, cols(i, u)],
                                                   ALU.subtract))
                    ch.restart()

            @block.scalar
            def _(e):
                ch = Chain(e, s["act"])
                with e.Fori(0, NSLAB) as i:
                    for u, (b0, nb) in enumerate(PARTS):
                        wait(e, s, f"stats{u}", i + 1)
                        e.activation(root[u][:, :], mv[u][:, :, 1], ACT.Sqrt, bias=self.eps[:, 0:1])\
                            .then_inc(s[f"root{u}"], 1)
                    for u, (b0, nb) in enumerate(PARTS):
                        wait(e, s, f"inv{u}", i + 1)
                        if to_hT:
                            wait(e, s, f"turned_h{u}", i)
                        for b in range(nb):
                            ch.add(e.activation(hN[u][:, b * P:(b + 1) * P],
                                                self.xN[:, bass.ds(i * SLAB + (b0 + b) * P, P)], ACT.Relu,
                                                scale=inv[u][:, b:b + 1], bias=off[u][:, b:b + 1]))
                        ch.sync()
                        e.sem_inc(s[f"normed{u}"])
                        if to_parts:
                            ch.add(e.copy(self.h3[:, 0, cols(i, u)], hN[u][:, :]))
                            ch.sync()
                            e.sem_inc(s[f"hi{u}"])
                    for u, (b0, nb) in enumerate(PARTS):
                        if to_parts:
                            wait(e, s, f"rest{u}", i + 1)
                            ch.add(e.copy(self.h3[:, 1, cols(i, u)], self.rest[u][:, :]))
                            ch.sync()
                            e.sem_inc(s[f"mid{u}"])
                    ch.restart()


    def to_nodes(self, w=None, out3=True, bias=None, column=None, column_bias=None, column_out=None):
        nc, ps = self.nc, self.ps
        names = ["passed", "dve", "act"] + pairs("cut", "hi", "mid")
        with stage(nc, *names, credited=pairs("made", "rest")) as (block, s):
            def cols(i, u):
                b0, nb = PARTS[u]
                return bass.ds(i * SLAB + b0 * P, nb * P)

            @block.gpsimd
            def _(e):
                with e.Fori(0, NSLAB) as i:
                    for u in (0, 1):
                        wait(e, s, f"made{u}", i)
                        e.tensor_copy(self.part[u][:, :], self.hT[:, cols(i, u)]).then_inc(s[f"cut{u}"], 1)

            @block.tensor
            def _(e):
                with e.Fori(0, NSLAB) as i:
                    for u, (_, nb) in enumerate(PARTS):
                        wait(e, s, f"cut{u}", i + 1)
                        wait(e, s, f"rest{u}", i)
                        for b in range(nb):
                            o = ps[:, u, b * P:(b + 1) * P]
                            piece = self.part[u][:, b * P:(b + 1) * P]
                            if w is None:
                                ins = e.transpose(o, piece, self.ident[:, :])
                            else:
                                ins = e.matmul(o, piece, w, start=True, stop=True)
                            if column is not None:
                                ins = e.matmul(ps[:, 2 + u, b:b + 1], piece, column, start=True, stop=True)
                        ins.then_inc(s[f"made{u}"], 1)

            @block.scalar
            def _(e):
                ch = Chain(e, s["act"])
                if out3:
                    with e.Fori(0, NSLAB) as i:
                        for u, (_, nb) in enumerate(PARTS):
                            wait(e, s, f"made{u}", i + 1)
                            ch.add(e.copy(self.h3[:, 0, cols(i, u)], ps[:, u, 0:nb * P]))
                            ch.sync()
                            e.sem_inc(s[f"hi{u}"])
                        for u, (_, nb) in enumerate(PARTS):
                            wait(e, s, f"rest{u}", i + 1)
                            ch.add(e.copy(self.h3[:, 1, cols(i, u)], self.rest[u][:, :]))
                            ch.sync()
                            e.sem_inc(s[f"mid{u}"])
                        ch.restart()

            @block.vector
            def _(e):
                ch = Chain(e, s["dve"])
                with e.Fori(0, NSLAB) as i:
                    for u, (b0, nb) in enumerate(PARTS):
                        if out3:
                            wait(e, s, f"hi{u}", i + 1)
                            ch.add(e.tensor_tensor(self.rest[u][:, :], ps[:, u, 0:nb * P], self.h3[:, 0, cols(i, u)],
                                                   ALU.subtract))
                        else:
                            wait(e, s, f"made{u}", i + 1)
                            out = self.msg[:, cols(i, u)].rearrange("p (b f) -> p b f", f=P)
                            b3 = bias.rearrange("p (a f) -> p a f", a=1).to_broadcast([P, nb, P])
                            ch.add(e.tensor_tensor(out, ps[:, u, 0:nb * P].rearrange("p (b f) -> p b f", f=P), b3, ALU.add))
                            if column is not None:
                                ch.add(e.tensor_scalar(column_out[:, bass.ds(i * SLAB_BLOCKS + b0, nb)],
                                                       ps[:, 2 + u, 0:nb], column_bias, None, ALU.add))
                        ch.sync()
                        e.sem_inc(s[f"rest{u}"])
                    for u, (_, nb) in enumerate(PARTS):
                        if out3:
                            wait(e, s, f"mid{u}", i + 1)
                            ch.add(e.tensor_tensor(self.h3[:, 2, cols(i, u)], self.rest[u][:, :], self.h3[:, 1, cols(i, u)],
                                                   ALU.subtract))
                    ch.restart()


    def stream_counts(self, e, s):
        table = self.count.rearrange("(s t) o -> s (t o)", t=PITCH)
        with e.Fori(0, 2) as half:
            with e.Fori(0, NB // SLOTS) as kk:
                for j in range(SLOTS):
                    wait(e, s, f"free{j}", half * (NB // SLOTS) + kk)
                    e.dma_start(self.ring[:, j, :],
                                table[bass.ds(kk * (SLOTS * P) + j * P, P), bass.ds(half * HALF, HALF)])\
                        .then_inc(s[f"slot{j}"], 16)
        for j in range(SLOTS):
            wait(e, s, f"free{j}", 2 * (NB // SLOTS))

    def aggregate(self, add_self=False):
        nc, ps = self.nc, self.ps
        turns = NB // SLOTS
        with stage(nc, "passed", *[f"slot{j}" for j in range(SLOTS)],
                   credited=[f"free{j}" for j in range(SLOTS)] + [f"out{c}" for c in range(HC)]) as (block, s):
            @block.sync
            def _(e):
                self.stream_counts(e, s)

            @block.tensor
            def _(e):
                with e.Fori(0, 2) as half:
                    for c in range(HC):
                        wait(e, s, f"out{c}", half)
                        e.matmul(ps[:, c, 0:CW], self.zero[:, 0:P], self.zero[:, :], start=True, stop=True)
                    with e.Fori(0, turns) as kk:
                        for j in range(SLOTS):
                            wait(e, s, f"slot{j}", half * (16 * turns) + kk * 16 + 16)
                            for part in range(3):
                                for c in range(HC):
                                    ins = e.matmul(ps[:, c, 0:CW], self.h3[:, part, bass.ds(kk * (SLOTS * P) + j * P, P)],
                                                   self.ring[:, j, c * CW:(c + 1) * CW], start=False, stop=True,
                                                   skip_group_check=True)
                            ins.then_inc(s[f"free{j}"], 1)

            def take(e, c, half):
                o = bass.ds(half * HALF + c * CW, CW)
                return o, self.aggT[:, o]

            @block.vector
            def _(e):
                with e.Fori(0, 2) as half:
                    wait(e, s, f"free{SLOTS - 1}", half * turns + turns)
                    for c in range(HC):
                        o, agg = take(e, c, half)
                        if add_self:
                            e.tensor_tensor(agg, ps[:, c, 0:CW], self.hT[:, o], ALU.add).then_inc(s[f"out{c}"], 1)
                        elif c % 2 == 0:
                            e.tensor_copy(agg, ps[:, c, 0:CW]).then_inc(s[f"out{c}"], 1)

            if not add_self:
                @block.scalar
                def _(e):
                    with e.Fori(0, 2) as half:
                        wait(e, s, f"free{SLOTS - 1}", half * turns + turns)
                        for c in range(1, HC, 2):
                            o, agg = take(e, c, half)
                            e.copy(agg, ps[:, c, 0:CW]).then_inc(s[f"out{c}"], 1)


    def dense(self, source, layers, target, first_relu=False):
        nc, ps = self.nc, self.ps
        L = len(layers)
        credited = pairs(*[f"mm{n}_" for n in range(L)], *[f"act{n}_" for n in range(1, L + 1)])
        with stage(nc, "passed", "act", *pairs("act0_"), credited=credited) as (block, s):
            mid = [[self.room(2 * n + u) for u in (0, 1)] for n in range(L)]

            def cols(i, u):
                return bass.ds(i * (2 * CW) + u * CW, CW)

            @block.tensor
            def _(e):
                with e.Fori(0, NCH // 2) as i:
                    for n, (w, _, _, _) in enumerate(layers):
                        for u in (0, 1):
                            if n > 0 or first_relu:
                                wait(e, s, f"act{n}_{u}", i + 1)
                            wait(e, s, f"act{n + 1}_{u}", i)
                            rhs = mid[n][u][:, :] if n > 0 or first_relu else source[:, cols(i, u)]
                            e.matmul(ps[:, 2 * n + u, 0:CW], w, rhs, start=True, stop=True).then_inc(s[f"mm{n}_{u}"], 1)

            @block.scalar
            def _(e):
                ch = Chain(e, s["act"])
                with e.Fori(0, NCH // 2) as i:
                    if first_relu:
                        for u in (0, 1):
                            wait(e, s, f"mm0_{u}", i)
                            ch.add(e.activation(mid[0][u][:, :], source[:, cols(i, u)], ACT.Relu))
                            ch.sync()
                            e.sem_inc(s[f"act0_{u}"])
                    for n, (_, func, scale, bias) in enumerate(layers):
                        for u in (0, 1):
                            wait(e, s, f"mm{n}_{u}", i + 1)
                            if n + 1 < L:
                                wait(e, s, f"mm{n + 1}_{u}", i)
                            out = mid[n + 1][u][:, :] if n + 1 < L else target[:, cols(i, u)]
                            ch.add(e.activation(out, ps[:, 2 * n + u, 0:CW], func, scale=scale, bias=bias))
                            ch.sync()
                            e.sem_inc(s[f"act{n + 1}_{u}"])
                    ch.restart()

    def gru(self, w_in, w_state, b_in, b_state, b_sum):
        nc, ps = self.nc, self.ps
        with stage(nc, "passed", "dve", "act", *pairs("mm", "rz", "new"), credited=pairs("pre", "next")) as (block, s):
            r, z, pre, new = [[self.room(2 * n + u) for u in (0, 1)] for n in range(4)]

            def cols(i, u):
                return bass.ds(i * (2 * CW) + u * CW, CW)

            @block.tensor
            def _(e):
                with e.Fori(0, NCH // 2) as i:
                    for u in (0, 1):
                        wait(e, s, f"pre{u}", i)
                        c, b = cols(i, u), 4 * u
                        for g in (0, 1):
                            e.matmul(ps[:, b + g, 0:CW], w_in[g], self.aggT[:, c], start=True, stop=False)
                            e.matmul(ps[:, b + g, 0:CW], w_state[g], self.hT[:, c], start=False, stop=True)
                        e.matmul(ps[:, b + 3, 0:CW], w_state[2], self.hT[:, c], start=True, stop=True)
                        e.matmul(ps[:, b + 2, 0:CW], w_in[2], self.aggT[:, c], start=True, stop=True)\
                            .then_inc(s[f"mm{u}"], 1)

            @block.scalar
            def _(e):
                ch = Chain(e, s["act"])
                with e.Fori(0, NCH // 2) as i:
                    for u in (0, 1):
                        wait(e, s, f"mm{u}", i + 1)
                        wait(e, s, f"next{u}", i)
                        ch.add(e.activation(r[u][:, :], ps[:, 4 * u, 0:CW], ACT.Sigmoid, bias=b_sum[0]))
                        ch.add(e.activation(z[u][:, :], ps[:, 4 * u + 1, 0:CW], ACT.Sigmoid, bias=b_sum[1]))
                        ch.sync()
                        e.sem_inc(s[f"rz{u}"])
                    for u in (0, 1):
                        wait(e, s, f"pre{u}", i + 1)
                        ch.add(e.activation(new[u][:, :], pre[u][:, :], ACT.Tanh, bias=b_in[2]))
                        ch.sync()
                        e.sem_inc(s[f"new{u}"])
                    ch.restart()

            @block.vector
            def _(e):
                ch = Chain(e, s["dve"])
                with e.Fori(0, NCH // 2) as i:
                    for u in (0, 1):
                        wait(e, s, f"rz{u}", i + 1)
                        ch.add(e.scalar_tensor_tensor(pre[u][:, :], ps[:, 4 * u + 3, 0:CW], b_state[2], r[u][:, :],
                                                      ALU.add, ALU.mult))
                        ch.sync()
                        ch.add(e.tensor_tensor(pre[u][:, :], ps[:, 4 * u + 2, 0:CW], pre[u][:, :], ALU.add))
                        ch.sync()
                        e.sem_inc(s[f"pre{u}"])
                    for u in (0, 1):
                        c = cols(i, u)
                        wait(e, s, f"new{u}", i + 1)
                        ch.add(e.tensor_tensor(self.hT[:, c], self.hT[:, c], new[u][:, :], ALU.subtract))
                        ch.sync()
                        ch.add(e.tensor_tensor(self.hT[:, c], self.hT[:, c], z[u][:, :], ALU.mult))
                        ch.sync()
                        ch.add(e.tensor_tensor(self.hT[:, c], self.hT[:, c], new[u][:, :], ALU.add))
                        ch.sync()
                        e.sem_inc(s[f"next{u}"])
                    ch.restart()


    def target_scores(self, w_rep, scores):
        nc, ps = self.nc, self.ps
        with stage(nc, "passed", *pairs("mm"), credited=pairs("out")) as (block, s):
            def cols(i, u):
                return bass.ds(i * (2 * CW) + u * CW, CW)

            @block.tensor
            def _(e):
                with e.Fori(0, NCH // 2) as i:
                    for u in (0, 1):
                        wait(e, s, f"out{u}", i)
                        e.matmul(ps[:, u, 0:CW], w_rep, self.hT[:, cols(i, u)], start=True, stop=True)\
                            .then_inc(s[f"mm{u}"], 1)

            @block.vector
            def _(e):
                with e.Fori(0, NCH // 2) as i:
                    for u in (0, 1):
                        wait(e, s, f"mm{u}", i + 1)
                        e.tensor_copy(scores[:, cols(i, u)], ps[:, u, 0:CW]).then_inc(s[f"out{u}"], 1)

    def attend(self, scores, source_scores, gate_room):
        nc, ps = self.nc, self.ps
        turns = NB // SLOTS
        R = 3
        names = ["passed", "cut"] + [f"slot{j}" for j in range(SLOTS)]\
            + [f"{n}{c}" for n in ("gate", "weighed") for c in range(HC)]
        credited = ["used_cut"] + [f"free{j}" for j in range(SLOTS)] + [f"{n}{c}" for n in ("out", "used") for c in range(HC)]
        with ExitStack() as tmp, stage(nc, *names, credited=credited) as (block, s):
            gate = gate_room.rearrange("p (c t) -> p c t", t=CW)
            piece = [scratch(nc, tmp, f"piece{b}", [P, P]) for b in range(2)]
            @block.sync
            def _(e):
                self.stream_counts(e, s)

            @block.gpsimd
            def _(e):
                with e.Fori(0, 2) as half:
                    with e.Fori(0, turns) as kk:
                        for j in range(SLOTS):
                            n = half * (NB) + kk * SLOTS + j
                            wait(e, s, "used_cut", n)
                            e.tensor_copy(piece[0][:, :], self.msg[:, bass.ds(kk * (SLOTS * P) + j * P, P)])\
                                .then_inc(s["cut"], 1)

            @block.scalar
            def _(e):
                with e.Fori(0, 2) as half:
                    with e.Fori(0, turns) as kk:
                        for j in range(SLOTS):
                            n = half * NB + kk * SLOTS + j
                            for c in range(HC):
                                wait(e, s, f"used{c}", n)
                                e.activation(gate[:, c, :], scores[:, bass.ds(half * HALF + c * CW, CW)], ACT.Sigmoid,
                                             bias=source_scores[:, bass.ds(kk * SLOTS + j, 1)])\
                                    .then_inc(s[f"gate{c}"], 1)

            @block.vector
            def _(e):
                with e.Fori(0, 2) as half:
                    with e.Fori(0, turns) as kk:
                        for j in range(SLOTS):
                            n = half * NB + kk * SLOTS + j
                            wait(e, s, f"slot{j}", half * (16 * turns) + kk * 16 + 16)
                            for c in range(HC):
                                wait(e, s, f"gate{c}", n + 1)
                                ins = e.tensor_tensor(gate[:, c, :], gate[:, c, :], self.ring[:, j, c * CW:(c + 1) * CW],
                                                      ALU.mult).then_inc(s[f"weighed{c}"], 1)
                            wait(e, s, f"weighed{HC - 1}", n + 1)
                            e.sem_inc(s[f"free{j}"])
                    wait(e, s, f"used{HC - 1}", half * NB + NB)
                    for c in range(HC):
                        e.tensor_copy(self.aggT[:, bass.ds(half * HALF + c * CW, CW)], ps[:, c, 0:CW])\
                            .then_inc(s[f"out{c}"], 1)

            @block.tensor
            def _(e):
                with e.Fori(0, 2) as half:
                    for c in range(HC):
                        wait(e, s, f"out{c}", half)
                        e.matmul(ps[:, c, 0:CW], self.zero[:, 0:P], self.zero[:, :], start=True, stop=True)
                    with e.Fori(0, turns) as kk:
                        for j in range(SLOTS):
                            n = half * NB + kk * SLOTS + j
                            wait(e, s, "cut", n + 1)
                            for c in range(HC):
                                wait(e, s, f"weighed{c}", n + 1)
                                ins = e.matmul(ps[:, c, 0:CW], piece[0][:, :], gate[:, c, :], start=False, stop=True,
                                               skip_group_check=True).then_inc(s[f"used{c}"], 1)
                            wait(e, s, f"used{HC - 1}", n + 1)
                            e.sem_inc(s["used_cut"])

    def batch_norm(self, gamma, beta):
        nc = self.nc
        W = 250
        assert N % W == 0
        with ExitStack() as tmp, stage(nc, "passed", "dve", "stats", "root", "inv", "done") as (block, s):
            def sb(n, shape):
                return scratch(nc, tmp, n, shape)
            stats, mv = sb("bn_st", [P, (N // W) * 6]), sb("bn_mv", [P, 2])
            root, inv, t, scale, shift = (sb(f"bn_{n}", [P, 1]) for n in ("root", "inv", "t", "scale", "shift"))

            @block.vector
            def _(e):
                ch = Chain(e, s["dve"])
                with e.Fori(0, N // W) as i:
                    e.bn_stats(stats[:, bass.ds(i * 6, 6)], self.hT[:, bass.ds(i * W, W)]).then_inc(s["stats"], 1)
                wait(e, s, "stats", N // W)
                ch.add(e.bn_aggr(mv[:, :], stats[:, :])); ch.sync()
                e.sem_inc(s["stats"])
                wait(e, s, "root", 1)
                self.rsqrt(ch, inv[:, :], mv[:, 1:2], root[:, :], t[:, :])
                ch.add(e.tensor_tensor(scale[:, :], gamma, inv[:, :], ALU.mult)); ch.sync()
                ch.add(e.scalar_tensor_tensor(shift[:, :], mv[:, 0:1], -1.0, scale[:, :], ALU.mult, ALU.mult)); ch.sync()
                ch.add(e.tensor_tensor(shift[:, :], shift[:, :], beta, ALU.add)); ch.sync()
                e.sem_inc(s["inv"])

            @block.scalar
            def _(e):
                wait(e, s, "stats", N // W + 1)
                e.activation(root[:, :], mv[:, 1:2], ACT.Sqrt, bias=self.eps[:, 0:1]).then_inc(s["root"], 1)
                wait(e, s, "inv", 1)
                with e.Fori(0, NSLAB) as i:
                    e.activation(self.hT[:, bass.ds(i * SLAB, SLAB)], self.hT[:, bass.ds(i * SLAB, SLAB)], ACT.Identity,
                                 scale=scale[:, 0:1], bias=shift[:, 0:1]).then_inc(s["done"], 1)
                wait(e, s, "done", NSLAB)


    def finish(self, out):
        nc, ps = self.nc, self.ps
        full = (N // P) * P
        with stage(nc, "passed", "store", *pairs("cut"), credited=pairs("turned", "added")) as (block, s):
            def cols(i, u):
                b0, nb = PARTS[u]
                return bass.ds(i * SLAB + b0 * P, nb * P)

            @block.gpsimd
            def _(e):
                with e.Fori(0, NSLAB) as i:
                    for u in (0, 1):
                        wait(e, s, f"turned{u}", i)
                        e.tensor_copy(self.part[u][:, :], self.hT[:, cols(i, u)]).then_inc(s[f"cut{u}"], 1)

            @block.tensor
            def _(e):
                with e.Fori(0, NSLAB) as i:
                    for u, (_, nb) in enumerate(PARTS):
                        wait(e, s, f"cut{u}", i + 1)
                        wait(e, s, f"added{u}", i)
                        for b in range(nb):
                            ins = e.transpose(ps[:, u, b * P:(b + 1) * P], self.part[u][:, b * P:(b + 1) * P],
                                              self.ident[:, :])
                        ins.then_inc(s[f"turned{u}"], 1)

            @block.vector
            def _(e):
                with e.Fori(0, NSLAB) as i:
                    for u, (b0, nb) in enumerate(PARTS):
                        wait(e, s, f"turned{u}", i + 1)
                        e.tensor_tensor(self.xN[:, cols(i, u)], ps[:, u, 0:nb * P], self.xN[:, cols(i, u)], ALU.add)\
                            .then_inc(s[f"added{u}"], 1)

            @block.sync
            def _(e):
                with e.Fori(0, NSLAB - 1) as i:
                    for u in (0, 1):
                        wait(e, s, f"added{u}", i + 1)
                    e.dma_start(out[bass.ds(i * SLAB, SLAB), :].rearrange("(k p) f -> p k f", p=P),
                                self.xN[:, bass.ds(i * SLAB, SLAB)].rearrange("p (k f) -> p k f", f=D))\
                        .then_inc(s["store"], 16)
                last = (NSLAB - 1) * SLAB
                for u in (0, 1):
                    wait(e, s, f"added{u}", NSLAB)
                e.dma_start(out[last:full, :].rearrange("(k p) f -> p k f", p=P),
                            self.xN[:, last:full].rearrange("p (k f) -> p k f", f=D)).then_inc(s["store"], 16)
                e.dma_start(out[full:N, :], self.xN[0:N - full, full:NP]).then_inc(s["store"], 16)
                wait(e, s, "store", 16 * (NSLAB + 1))


def program(nc, a, out):
    count = nc.dram_tensor("count", [(NP + 1) * PITCH, 1], BF16, kind="Internal").ap()
    build_counts(nc, a["src"], a["dst"], count)

    with ExitStack() as ctx:
        net = Net(nc, ctx, count)
        sb = net.sb

        def gates(m):
            return [m[g * D:(g + 1) * D, :] for g in range(3)]

        names, matrices = {}, []
        for key, blocks in (("1ih", gates(a["L1_gnn_W_ih"])), ("1hh", gates(a["L1_gnn_W_hh"])),
                            ("2e1", [a["L2_gnn_enc_w1"]]), ("2e2", [a["L2_gnn_enc_w2"]]),
                            ("2ih", gates(a["L2_gnn_gru_wih"])), ("2hh", gates(a["L2_gnn_gru_whh"])),
                            ("2d1", [a["L2_gnn_dec_w1"]]), ("2d2", [a["L2_gnn_dec_w2"]]), ("3", [a["L3_gnn_W"]])):
            names[key] = range(len(matrices), len(matrices) + len(blocks))
            matrices += blocks

        def column(v):
            return v.rearrange("(p o) -> p o", o=1)

        def three(v):
            return v.rearrange("(g p) -> p g", p=P)

        b1i, b1h, b1s = sb("b1i", [P, 3]), sb("b1h", [P, 3]), sb("b1s", [P, 3])
        b2i, b2h, b2s = sb("b2i", [P, 3]), sb("b2h", [P, 3]), sb("b2s", [P, 3])
        gam, bet, e1, e2, d1, d2, b3 = (sb(n, [P, 1]) for n in ("gam", "bet", "e1", "e2", "d1", "d2", "b3"))
        w_att = sb("w_att", [P, 2])
        b_att = sb("b_att", [P, 1])
        b_msg = sb("b_msg", [P, D])
        w_msg = sb("w_msg", [P, D])
        att_rep = sb("att_rep", [P, P])
        vectors = [(b1i[:, :], three(a["L1_gnn_b_ih"])), (b1h[:, :], three(a["L1_gnn_b_hh"])),
                   (b2i[:, :], three(a["L2_gnn_gru_bih"])), (b2h[:, :], three(a["L2_gnn_gru_bhh"])),
                   (gam[:, :], column(a["L1_gnn_gamma"])), (bet[:, :], column(a["L1_gnn_beta"])),
                   (e1[:, :], column(a["L2_gnn_enc_b1"])), (e2[:, :], column(a["L2_gnn_enc_b2"])),
                   (d1[:, :], column(a["L2_gnn_dec_b1"])), (d2[:, :], column(a["L2_gnn_dec_b2"])),
                   (b3[:, :], column(a["L3_gnn_b"])),
                   (w_att[:, :], a["L1_gnn_W_att"].rearrange("(g p) o -> p (g o)", p=P)),
                   (b_att[:, :], a["L1_gnn_b_att"].rearrange("(a o) -> a o", a=1).to_broadcast([P, 1]))]
        directs = [(b_msg[:, :], a["L1_gnn_b_msg"].rearrange("(a f) -> a f", a=1).to_broadcast([P, D])),
                   (w_msg[:, :], a["L1_gnn_W_msg"])]
        net.setup(a["x"], matrices, vectors, directs)

        def wt(key):
            return [net.wT[:, i, :] for i in names[key]]

        with stage(nc, "one") as (block, s):
            @block.vector
            def _(e):
                e.tensor_tensor(b1s[:, :], b1i[:, :], b1h[:, :], ALU.add).then_inc(s["one"], 1)
                e.tensor_tensor(b2s[:, :], b2i[:, :], b2h[:, :], ALU.add).then_inc(s["one"], 1)
                e.tensor_copy(att_rep[:, :], w_att[:, 1:2].to_broadcast([P, P])).then_inc(s["one"], 1)
                wait(e, s, "one", 3)

        net.norm(add=False, to_hT=True, to_parts=True)
        w12 = sb("w12", [P, 2, D])
        vec = sb("vec", [P, 5, 2])
        bn = sb("bn", [P, 4, 2])
        layers0 = 3
        with nc.Fori(0, layers0) as layer:
            with stage(nc, "w", "root", "var", "dve") as (block, s):
                @block.sync
                def _(e):
                    for n, m in enumerate((a["L0_gnn_W1"], a["L0_gnn_W2"])):
                        e.dma_start(w12[:, n, :], m.rearrange("l i o -> (l i) o")[bass.ds(layer * D, D), :])\
                            .then_inc(s["w"], 16)
                    with nc.allow_non_contiguous_dma(reason="vectors of 128 words, one to a partition"):
                        for n, v in enumerate((a["L0_gnn_b1"], a["L0_gnn_b2"])):
                            e.dma_start(vec[:, 0, n:n + 1],
                                        v.rearrange("l (f o) -> (l f) o", o=1)[bass.ds(layer * D, D), :])\
                                .then_inc(s["w"], 16)
                        for q, v in enumerate((a["L0_gnn_g"], a["L0_gnn_be"], a["L0_gnn_rm"], a["L0_gnn_rv"])):
                            for n in (0, 1):
                                e.dma_start(vec[:, 1 + q, n:n + 1],
                                            v.rearrange("l n (f o) -> (l n f) o", o=1)[bass.ds(layer * (2 * D) + n * D, D), :])\
                                    .then_inc(s["w"], 16)
                    wait(e, s, "w", 12 * 16)

                @block.scalar
                def _(e):
                    wait(e, s, "w", 12 * 16)
                    e.activation(bn[:, 0, :], vec[:, 4, :], ACT.Sqrt, bias=net.eps[:, 0:1]).then_inc(s["root"], 1)

                @block.vector
                def _(e):
                    ch = Chain(e, s["dve"])
                    wait(e, s, "root", 1)
                    net.rsqrt(ch, bn[:, 1, :], vec[:, 4, :], bn[:, 0, :], bn[:, 2, :])
                    ch.add(e.tensor_tensor(bn[:, 1, :], bn[:, 1, :], vec[:, 1, :], ALU.mult)); ch.sync()
                    ch.add(e.tensor_tensor(bn[:, 3, :], vec[:, 0, :], vec[:, 3, :], ALU.subtract)); ch.sync()
                    ch.add(e.tensor_tensor(bn[:, 3, :], bn[:, 3, :], bn[:, 1, :], ALU.mult)); ch.sync()
                    ch.add(e.tensor_tensor(bn[:, 3, :], bn[:, 3, :], vec[:, 2, :], ALU.add)); ch.sync()
            net.aggregate(add_self=True)
            net.dense(net.aggT, [(w12[:, n, :], ACT.Relu, bn[:, 1, n:n + 1], bn[:, 3, n:n + 1]) for n in (0, 1)], net.hT)
            net.to_nodes()

        net.norm(add=True, to_hT=True, to_parts=False)
        source_scores = sb("source_scores", [P, NB])
        scores = net.h3[:, 0:2, :].rearrange("p a t -> p (a t)").bitcast(F32)
        net.to_nodes(w_msg[:, :], out3=False, bias=b_msg[:, :], column=w_att[:, 0:1], column_bias=b_att[:, 0:1],
                     column_out=source_scores)
        net.target_scores(att_rep[:, :], scores)
        net.attend(scores, source_scores, net.h3[:, 2, :].bitcast(F32))
        net.gru(wt("1ih"), wt("1hh"), [b1i[:, g:g + 1] for g in range(3)], [b1h[:, g:g + 1] for g in range(3)],
                [b1s[:, g:g + 1] for g in range(3)])
        net.batch_norm(gam[:, :], bet[:, :])

        net.norm(add=True, to_hT=True, to_parts=False)
        net.dense(net.hT, [(wt("2e1")[0], ACT.Relu, 1.0, e1[:, :]), (wt("2e2")[0], ACT.Identity, 1.0, e2[:, :])], net.hT)
        w_step = sb("w_step", [P, D])
        steps = 5
        with nc.Fori(0, steps) as step:
            with stage(nc, "w") as (block, s):
                @block.sync
                def _(e):
                    e.dma_start(w_step[:, :], a["L2_gnn_conv_w"].rearrange("l i o -> (l i) o")[bass.ds(step * D, D), :])\
                        .then_inc(s["w"], 16)
                    wait(e, s, "w", 16)
            net.to_nodes(w_step[:, :])
            net.aggregate()
            net.gru(wt("2ih"), wt("2hh"), [b2i[:, g:g + 1] for g in range(3)], [b2h[:, g:g + 1] for g in range(3)],
                    [b2s[:, g:g + 1] for g in range(3)])
        net.dense(net.hT, [(wt("2d1")[0], ACT.Relu, 1.0, d1[:, :]), (wt("2d2")[0], ACT.Sigmoid, 1.0, d2[:, :])], net.hT,
                  first_relu=True)

        net.norm(add=True, to_hT=False, to_parts=True)
        net.aggregate()
        net.dense(net.aggT, [(wt("3")[0], ACT.Identity, 1.0, b3[:, :])], net.hT)
        net.finish(out)


def kernel(**inputs):
    import concourse.bacc as bacc
    from concourse.bass_utils import run_bass_kernel_spmd

    nc = bacc.Bacc("TRN2", target_bir_lowering=False, num_devices=1)
    arrays, aps = {}, {}
    for name, value in inputs.items():
        value = np.ascontiguousarray(value)
        arrays[f"in_{name}"] = value
        aps[name] = nc.dram_tensor(f"in_{name}", value.shape, mybir.dt.from_np(value.dtype), kind="ExternalInput").ap()
    out = nc.dram_tensor("out", (N, D), F32, kind="ExternalOutput").ap()
    program(nc, aps, out)
    result = run_bass_kernel_spmd(nc, [arrays], core_ids=[0])
    return np.asarray(result.results[0]["out"])
```

```python
from contextlib import ExitStack, contextmanager

import numpy as np

import concourse.bass as bass
from concourse import mybir

F32 = mybir.dt.float32
BF16 = mybir.dt.bfloat16
F16 = mybir.dt.float16
I32 = mybir.dt.int32
U32 = mybir.dt.uint32
ALU = mybir.AluOpType
ACT = mybir.ActivationFunctionType

N = 6250
E = 100000
D = 128
P = 128
NB = -(-N // P)
NP = NB * P
SLAB_BLOCKS = 7
NSLAB = NB // SLAB_BLOCKS
SLAB = SLAB_BLOCKS * P
CW = 448
NCH = NP // CW
HC = NCH // 2
HALF = HC * CW
SLOTS = 7
LN_EPS = 1e-5
assert NB % SLAB_BLOCKS == 0 and NP % CW == 0 and NCH % 2 == 0 and SLAB == 2 * CW and NB % SLOTS == 0

PARTS = [(0, 4), (4, 3)]

SRC_SHIFT = 13
PITCH = 1 << SRC_SHIFT
KEY_BASE = 0x20000000
KEY_MASK = KEY_BASE - 1
GROUP = 8
TROWS = 112
TCH = 7
NT = TROWS * TCH
NG = NT // GROUP
GW = GROUP * P
FULL_T, TAIL = divmod(E, P)
assert NT * P >= E and NP <= PITCH and NG % 2 == 0
FIRST_MARK = 2048
PAD_TARGET = 1024


class Semaphores(dict):
    credited = frozenset()


@contextmanager
def stage(nc, *names, credited=()):
    s = Semaphores((n, nc.alloc_semaphore(f"{n}_{nc.next_id()}")) for n in (*names, *credited))
    s.credited = frozenset(credited)
    for name in credited:
        nc.gpsimd.sem_inc(s[name])
    if credited:
        nc.all_engine_barrier()
    with nc.Block() as block:
        yield block, s
    nc.clear_and_free_semaphores(list(s.values()))
    nc.all_engine_barrier()


def pairs(*names):
    return [f"{n}{u}" for n in names for u in (0, 1)]


def wait(engine, s, name, value):
    engine.wait_ge(s[name], value + (name in s.credited))
    if not isinstance(value, int):
        engine.sem_inc(s["passed"])


def scratch(nc, ctx, name, shape, dt=F32):
    return ctx.enter_context(nc.sbuf_tensor(f"{name}_{nc.next_id()}", shape, dt))


class Chain:

    def __init__(self, engine, sem):
        self.engine, self.sem, self.n = engine, sem, 0

    def add(self, instruction):
        instruction.then_inc(self.sem, 1)
        self.n += 1
        return instruction

    def sync(self):
        self.engine.wait_ge(self.sem, self.n)

    def restart(self):
        self.sync()
        self.engine.sem_clear(self.sem)
        self.n = 0


def build_counts(nc, src, dst, count):
    keyrow = nc.dram_tensor("keyrow", [NT * P], F32, kind="Internal").ap()
    with ExitStack() as ctx:
        def sb(name, shape, dt):
            return ctx.enter_context(nc.sbuf_tensor(name, shape, dt))

        ident = sb("b_ident", [P, P], F32)
        s_rows = sb("s_rows", [TROWS, TCH, P], I32)
        d_rows = sb("d_rows", [TROWS, TCH, P], I32)
        key_rows = sb("key_rows", [TROWS, TCH, P], I32)
        keyT = sb("keyT", [P, NT], F32)
        zeros = sb("zeros", [P, NP], F16)
        order_i = sb("order_i", [P, GROUP, GW], I32)
        weight = sb("weight", [P, GROUP, GW], F32)
        dump_i = sb("dump_i", [P, GROUP], I32)
        dump = sb("dump", [P, GROUP], I32)
        rows = [sb(f"rows{b}", [P, GW], F32) for b in (0, 1)]
        junk = sb("junk", [P, GROUP, GW], BF16)
        acc = sb("acc", [P, GROUP], F32)
        repeated = sb("repeated", [P, GROUP], U32)
        where = sb("where", [P, GROUP], I32)
        index = [sb(f"index{b}", [P, GROUP], U32) for b in (0, 1)]
        amount = [sb(f"amount{b}", [P, GROUP], F16) for b in (0, 1)]
        ps = ctx.enter_context(nc.psum_tensor("b_ps", [P, 2, 512], F32))

        with stage(nc, "pad", "edges", "id0", "id1", "ord", "dve", "keys", "tr", "kout") as (block, s):
            whole = (TCH - 1) * TROWS

            @block.gpsimd
            def _(e):
                e.memset(ident[:, :], 0.0).then_inc(s["id0"], 1)
                wait(e, s, "id0", 1)
                e.affine_select(out=ident[:, :], in_=ident[:, :], compare_op=ALU.not_equal, fill=1.0, base=0,
                                pattern=[[-1, P]], channel_multiplier=1).then_inc(s["id1"], 1)
                e.iota(order_i[:, :, :], pattern=[[P, GROUP], [-1, GW]], base=0, channel_multiplier=1)\
                    .then_inc(s["ord"], 1)
                e.iota(dump_i[:, :], pattern=[[P, GROUP]], base=NP << SRC_SHIFT, channel_multiplier=1)\
                    .then_inc(s["ord"], 1)

            @block.sync
            def _(e):
                for n, (edges, tile) in enumerate(((src, s_rows), (dst, d_rows))):
                    e.dma_start(tile[:, 0:TCH - 1, :], edges[0:whole * P].rearrange("(c p l) -> p c l", p=TROWS, l=P))\
                        .then_inc(s["edges"], 16)
                    wait(e, s, "pad", 2 * n + 2)
                    e.dma_start(tile[0:FULL_T - whole, TCH - 1, :],
                                edges[whole * P:FULL_T * P].rearrange("(p l) -> p l", l=P)).then_inc(s["edges"], 16)
                    e.dma_start(tile[FULL_T - whole:FULL_T - whole + 1, TCH - 1, 0:TAIL],
                                edges[FULL_T * P:E].rearrange("(a l) -> a l", a=1)).then_inc(s["edges"], 16)
                wait(e, s, "keys", 1)
                e.dma_start(keyrow.rearrange("(c p l) -> p c l", p=TROWS, l=P), key_rows[:, :, :].bitcast(F32))\
                    .then_inc(s["kout"], 16)
                wait(e, s, "kout", 16)

            @block.vector
            def _(e):
                ch = Chain(e, s["dve"])
                for tile, value in ((s_rows, NP), (d_rows, PAD_TARGET)):
                    e.memset(tile[:, TCH - 1, :], value).then_inc(s["pad"], 2)
                ch.add(e.memset(zeros[:, :], 0.0))
                wait(e, s, "ord", 2)
                ch.add(e.tensor_scalar(weight[:, :, :], order_i[:, :, :], 0.0, float(FIRST_MARK), ALU.is_gt, ALU.mult))
                ch.add(e.tensor_scalar(dump[:, :], dump_i[:, :], KEY_BASE, None, ALU.bitwise_or))
                ch.sync()
                ch.add(e.tensor_scalar(weight[:, :, :], weight[:, :, :], 1.0, None, ALU.add))
                wait(e, s, "edges", 6 * 16)
                ch.add(e.tensor_scalar(key_rows[:, :, :], s_rows[:, :, :], SRC_SHIFT, KEY_BASE,
                                       ALU.logical_shift_left, ALU.bitwise_or))
                ch.sync()
                e.tensor_tensor(key_rows[:, :, :], key_rows[:, :, :], d_rows[:, :, :], ALU.bitwise_or)\
                    .then_inc(s["keys"], 1)
                for c in range(TCH):
                    wait(e, s, "tr", c + 1)
                    ch.add(e.tensor_copy(keyT[:, c * TROWS:(c + 1) * TROWS], ps[:, c % 2, 0:TROWS]))
                ch.sync()

            @block.tensor
            def _(e):
                wait(e, s, "keys", 1)
                wait(e, s, "id1", 1)
                for c in range(TCH):
                    if c >= 2:
                        wait(e, s, "dve", 5 + c - 1)
                    e.transpose(ps[:, c % 2, 0:TROWS], key_rows[:, c, :].bitcast(F32), ident[0:TROWS, 0:TROWS])\
                        .then_inc(s["tr"], 1)

        table = count.rearrange("(s t) o -> s (t o)", t=PITCH)
        with stage(nc, "zero", "dve", "landed", "passed", *pairs("load", "made"),
                   credited=pairs("used", "freed")) as (block, s):
            @block.sync
            def _(e):
                e.dma_start(table[NP:NP + 1, :].rearrange("a (p t) -> (a p) t", p=16), zeros[0:16, 0:PITCH // 16])\
                    .then_inc(s["zero"], 16)
                with e.Fori(0, NB) as k:
                    e.dma_start(table[bass.ds(k * P, P), 0:NP], zeros[:, :]).then_inc(s["zero"], 16)
                with e.Fori(0, NG // 2) as i:
                    for b in (0, 1):
                        wait(e, s, f"used{b}", i)
                        e.dma_start(rows[b][:, :], keyrow[bass.ds(i * (2 * GW) + b * GW, GW)]
                                    .rearrange("(a l) -> a l", a=1).to_broadcast([P, GW]))\
                            .then_inc(s[f"load{b}"], 16)
                wait(e, s, "used0", NG // 2)
                wait(e, s, "used1", NG // 2)

            @block.vector
            def _(e):
                ch = Chain(e, s["dve"])
                with e.Fori(0, NG // 2) as i:
                    for b in (0, 1):
                        wait(e, s, f"load{b}", i * 16 + 16)
                        col = i * (2 * GROUP) + b * GROUP
                        for t in range(GROUP):
                            ch.add(e.scalar_tensor_tensor(
                                junk[:, t, :], rows[b][:, :], keyT[:, bass.ds(col + t, 1)],
                                weight[:, t, :], ALU.is_equal, ALU.mult, accum_out=acc[:, t:t + 1]))
                        ch.add(e.tensor_copy(where[:, :], keyT[:, bass.ds(col, GROUP)].bitcast(I32)))
                        ch.sync()
                        e.sem_inc(s[f"used{b}"])
                        ch.add(e.tensor_scalar(repeated[:, :], acc[:, :], FIRST_MARK - 0.5, None, ALU.is_gt))
                        ch.sync()
                        ch.add(e.copy_predicated(where[:, :], repeated[:, :], dump[:, :]))
                        ch.sync()
                        wait(e, s, f"freed{b}", i)
                        ch.add(e.scalar_tensor_tensor(amount[b][:, :], acc[:, :], FIRST_MARK - 0.5, acc[:, :],
                                                      ALU.is_lt, ALU.mult))
                        ch.add(e.tensor_scalar(index[b][:, :], where[:, :].bitcast(U32), KEY_MASK, None,
                                               ALU.bitwise_and))
                        ch.sync()
                        e.sem_inc(s[f"made{b}"])
                    ch.restart()

            @block.gpsimd
            def _(e):
                e.wait_ge(s["zero"], 16 * (NB + 1))
                with e.Fori(0, NG // 2) as i:
                    for b in (0, 1):
                        wait(e, s, f"made{b}", i + 1)
                        for t in range(GROUP):
                            e.indirect_dma_start(
                                out=count, out_offset=bass.IndirectOffsetOnAxis(ap=index[b][:, t:t + 1], axis=0),
                                in_=amount[b][:, t:t + 1], in_offset=None, compute_op=ALU.add)\
                                .then_inc(s["landed"], 16)
                        wait(e, s, "landed", i * (2 * GROUP * 16) + (b + 1) * GROUP * 16)
                        e.sem_inc(s[f"freed{b}"])


class Net:

    def __init__(self, nc, ctx, count):
        self.nc, self.ctx, self.count = nc, ctx, count
        sb = self.sb
        self.hT = sb("hT", [P, NP])
        self.aggT = sb("aggT", [P, NP])
        self.xN = sb("xN", [P, NP])
        self.h3 = sb("h3", [P, 3, NP], BF16)
        self.msg = sb("msg", [P, NP])
        self.ring = sb("ring", [P, SLOTS, HALF], F16)
        self.ident = sb("ident", [P, P])
        self.zero = sb("zero", [P, CW], BF16)
        self.eps = sb("eps", [P, 1])
        self.part = [sb(f"part{u}", [P, nb * P]) for u, (_, nb) in enumerate(PARTS)]
        self.rest = [sb(f"rest{u}", [P, nb * P]) for u, (_, nb) in enumerate(PARTS)]
        self.ps = ctx.enter_context(nc.psum_tensor("ps", [P, 8, 512], F32))

    def sb(self, name, shape, dt=F32):
        return self.ctx.enter_context(self.nc.sbuf_tensor(name, shape, dt))

    def room(self, n):
        return self.h3[:, :, :].rearrange("p a t -> p (a t)").bitcast(F32)[:, n * CW:(n + 1) * CW]


    def setup(self, x, matrices, vectors, directs):
        nc, P_ = self.nc, P
        full = (N // P) * P
        nm = len(matrices)
        self.wT = self.sb("wT", [P, nm, P])
        with ExitStack() as tmp:
            raw = self.ring[:, 0:3, :].rearrange("p s t -> p (s t)").bitcast(F32)[:, 0:nm * P]\
                .rearrange("p (m t) -> p m t", t=P)
            with stage(nc, "id0", "cst", "x0", "x1", "w", "v", "tr", "cp") as (block, s):
                @block.gpsimd
                def _(e):
                    e.memset(self.ident[:, :], 0.0).then_inc(s["id0"], 1)
                    wait(e, s, "id0", 1)
                    e.affine_select(out=self.ident[:, :], in_=self.ident[:, :], compare_op=ALU.not_equal, fill=1.0,
                                    base=0, pattern=[[-1, P]], channel_multiplier=1).then_inc(s["cst"], 1)
                    e.memset(self.zero[:, :], 0.0).then_inc(s["cst"], 1)
                    e.memset(self.eps[:, :], LN_EPS).then_inc(s["cst"], 1)
                    wait(e, s, "cst", 3)

                @block.sync
                def _(e):
                    e.dma_start(self.xN[:, 0:full].rearrange("p (k f) -> p k f", f=D),
                                x[0:full, :].rearrange("(k p) f -> p k f", p=P)).then_inc(s["x1"], 16)
                    for i, m in enumerate(matrices):
                        e.dma_start(raw[:, i, :], m).then_inc(s["w"], 16)
                    wait(e, s, "x0", 1)
                    e.dma_start(self.xN[0:N - full, full:NP], x[full:N, :]).then_inc(s["x1"], 16)
                    with nc.allow_non_contiguous_dma(reason="vectors of 128 words, one to a partition"):
                        for tile, v in vectors:
                            e.dma_start(tile, v).then_inc(s["v"], 16)
                    for tile, v in directs:
                        e.dma_start(tile, v).then_inc(s["v"], 16)
                    wait(e, s, "x1", 32)
                    wait(e, s, "v", 16 * (len(vectors) + len(directs)))

                @block.vector
                def _(e):
                    e.memset(self.xN[:, full:NP], 0.0).then_inc(s["x0"], 1)
                    for i in range(nm):
                        wait(e, s, "tr", i + 1)
                        e.tensor_copy(self.wT[:, i, :], self.ps[:, i % 8, 0:P]).then_inc(s["cp"], 1)
                    wait(e, s, "cp", nm)

                @block.tensor
                def _(e):
                    wait(e, s, "cst", 3)
                    wait(e, s, "w", 16 * nm)
                    for i in range(nm):
                        if i >= 8:
                            wait(e, s, "cp", i - 7)
                        e.transpose(self.ps[:, i % 8, 0:P], raw[:, i, :], self.ident[:, :]).then_inc(s["tr"], 1)

    @staticmethod
    def rsqrt(ch, y, var, root, t):
        e = ch.engine
        ch.add(e.reciprocal(y, root)); ch.sync()
        ch.add(e.tensor_tensor(t, y, y, ALU.mult)); ch.sync()
        ch.add(e.scalar_tensor_tensor(t, var, LN_EPS, t, ALU.add, ALU.mult)); ch.sync()
        ch.add(e.tensor_scalar(t, t, -0.5, 1.5, ALU.mult, ALU.add)); ch.sync()
        ch.add(e.tensor_tensor(y, y, t, ALU.mult)); ch.sync()


    def norm(self, add):
        nc, ps = self.nc, self.ps
        names = ["passed", "dve", "stats", "root"] + pairs("cut", "normed")
        credited = pairs(*["turned", "added"] * add, "turned_h", "stored")
        with ExitStack() as tmp, stage(nc, *names, credited=credited) as (block, s):
            stats = [scratch(nc, tmp, f"stats{u}", [P, nb, 6]) for u, (_, nb) in enumerate(PARTS)]
            mv_slab = scratch(nc, tmp, "mv_slab", [P, SLAB_BLOCKS, 2])
            mv = scratch(nc, tmp, "mv", [P, 2 * NB])
            mean, var = (mv[:, :].rearrange("p (k t) -> p k t", t=2)[:, :, n] for n in (0, 1))
            root = scratch(nc, tmp, "root", [P, NB])
            inv = scratch(nc, tmp, "inv", [P, NB])
            tmp1 = scratch(nc, tmp, "tmp1", [P, NB])

            def cols(i, u):
                b0, nb = PARTS[u]
                return bass.ds(i * SLAB + b0 * P, nb * P)

            if add:
                @block.gpsimd
                def _(e):
                    with e.Fori(0, NSLAB) as i:
                        for u in (0, 1):
                            wait(e, s, f"turned{u}", i)
                            e.tensor_copy(self.part[u][:, :], self.hT[:, cols(i, u)]).then_inc(s[f"cut{u}"], 1)

            @block.tensor
            def _(e):
                if add:
                    with e.Fori(0, NSLAB) as i:
                        for u, (_, nb) in enumerate(PARTS):
                            wait(e, s, f"cut{u}", i + 1)
                            wait(e, s, f"added{u}", i)
                            for b in range(nb):
                                ins = e.transpose(ps[:, u, b * P:(b + 1) * P], self.part[u][:, b * P:(b + 1) * P],
                                                  self.ident[:, :])
                            ins.then_inc(s[f"turned{u}"], 1)
                with e.Fori(0, NSLAB) as i:
                    for u, (_, nb) in enumerate(PARTS):
                        wait(e, s, f"normed{u}", i + 1)
                        wait(e, s, f"stored{u}", i)
                        for b in range(nb):
                            ins = e.transpose(ps[:, 2 + u, b * P:(b + 1) * P], self.rest[u][:, b * P:(b + 1) * P],
                                              self.ident[:, :])
                        ins.then_inc(s[f"turned_h{u}"], 1)

            @block.vector
            def _(e):
                ch = Chain(e, s["dve"])
                with e.Fori(0, NSLAB) as i:
                    if add:
                        for u, (b0, nb) in enumerate(PARTS):
                            wait(e, s, f"turned{u}", i + 1)
                            ch.add(e.tensor_tensor(self.xN[:, cols(i, u)], ps[:, u, 0:nb * P], self.xN[:, cols(i, u)],
                                                   ALU.add))
                        ch.sync()
                        for u in (0, 1):
                            e.sem_inc(s[f"added{u}"])
                    for u, (b0, nb) in enumerate(PARTS):
                        for b in range(nb):
                            ch.add(e.bn_stats(stats[u][:, b, :], self.xN[:, bass.ds(i * SLAB + (b0 + b) * P, P)]))
                    ch.sync()
                    for u, (b0, nb) in enumerate(PARTS):
                        for b in range(nb):
                            ch.add(e.bn_aggr(mv_slab[:, b0 + b, :], stats[u][:, b, :]))
                    ch.sync()
                    ch.add(e.tensor_copy(mv[:, bass.ds(i * (2 * SLAB_BLOCKS), 2 * SLAB_BLOCKS)],
                                         mv_slab[:, :, :].rearrange("p b t -> p (b t)")))
                    ch.restart()
                e.sem_inc(s["stats"])
                e.wait_ge(s["root"], 1)
                self.rsqrt(ch, inv[:, :], var, root[:, :], tmp1[:, :])
                ch.restart()
                with e.Fori(0, NSLAB) as i:
                    for u, (b0, nb) in enumerate(PARTS):
                        wait(e, s, f"turned_h{u}", i)
                        for b in range(nb):
                            k = i * SLAB_BLOCKS + b0 + b
                            ch.add(e.tensor_scalar(self.rest[u][:, b * P:(b + 1) * P],
                                                   self.xN[:, bass.ds(i * SLAB + (b0 + b) * P, P)],
                                                   mv[:, bass.ds(k * 2, 1)], inv[:, bass.ds(k, 1)],
                                                   ALU.subtract, ALU.mult))
                        ch.sync()
                        e.sem_inc(s[f"normed{u}"])
                    ch.restart()

            @block.scalar
            def _(e):
                e.wait_ge(s["stats"], 1)
                e.activation(root[:, :], var, ACT.Sqrt, bias=self.eps[:, 0:1]).then_inc(s["root"], 1)
                with e.Fori(0, NSLAB) as i:
                    for u, (b0, nb) in enumerate(PARTS):
                        wait(e, s, f"turned_h{u}", i + 1)
                        e.activation(self.hT[:, cols(i, u)], ps[:, 2 + u, 0:nb * P], ACT.Relu)\
                            .then_inc(s[f"stored{u}"], 1)


    def messages(self, w, bias, column, column_bias, column_out):
        nc, ps = self.nc, self.ps
        with stage(nc, "passed", "dve", *pairs("cut"), credited=pairs("made", "taken")) as (block, s):
            def cols(i, u):
                b0, nb = PARTS[u]
                return bass.ds(i * SLAB + b0 * P, nb * P)

            @block.gpsimd
            def _(e):
                with e.Fori(0, NSLAB) as i:
                    for u in (0, 1):
                        wait(e, s, f"made{u}", i)
                        e.tensor_copy(self.part[u][:, :], self.hT[:, cols(i, u)]).then_inc(s[f"cut{u}"], 1)

            @block.tensor
            def _(e):
                with e.Fori(0, NSLAB) as i:
                    for u, (_, nb) in enumerate(PARTS):
                        wait(e, s, f"cut{u}", i + 1)
                        wait(e, s, f"taken{u}", i)
                        for b in range(nb):
                            piece = self.part[u][:, b * P:(b + 1) * P]
                            e.matmul(ps[:, u, b * P:(b + 1) * P], piece, w, start=True, stop=True)
                            ins = e.matmul(ps[:, 2 + u, b:b + 1], piece, column, start=True, stop=True)
                        ins.then_inc(s[f"made{u}"], 1)

            @block.vector
            def _(e):
                ch = Chain(e, s["dve"])
                with e.Fori(0, NSLAB) as i:
                    for u, (b0, nb) in enumerate(PARTS):
                        wait(e, s, f"made{u}", i + 1)
                        out = self.msg[:, cols(i, u)].rearrange("p (b f) -> p b f", f=P)
                        b3 = bias.rearrange("p (a f) -> p a f", a=1).to_broadcast([P, nb, P])
                        ch.add(e.tensor_tensor(out, ps[:, u, 0:nb * P].rearrange("p (b f) -> p b f", f=P), b3, ALU.add))
                        ch.add(e.tensor_scalar(column_out[:, bass.ds(i * SLAB_BLOCKS + b0, nb)],
                                               ps[:, 2 + u, 0:nb], column_bias, None, ALU.add))
                        ch.sync()
                        e.sem_inc(s[f"taken{u}"])
                    ch.restart()


    def stream_counts(self, e, s):
        table = self.count.rearrange("(s t) o -> s (t o)", t=PITCH)
        with e.Fori(0, 2) as half:
            with e.Fori(0, NB // SLOTS) as kk:
                for j in range(SLOTS):
                    wait(e, s, f"free{j}", half * (NB // SLOTS) + kk)
                    e.dma_start(self.ring[:, j, :],
                                table[bass.ds(kk * (SLOTS * P) + j * P, P), bass.ds(half * HALF, HALF)])\
                        .then_inc(s[f"slot{j}"], 16)
        for j in range(SLOTS):
            wait(e, s, f"free{j}", 2 * (NB // SLOTS))

    def aggregate(self, w=None, add_self=False, load=(), prepare_act=None, prepare_dve=None):
        nc, ps = self.nc, self.ps
        turns = NB // SLOTS
        assert SLOTS == SLAB_BLOCKS and HC == 7
        SPARE = 7
        with stage(nc, "passed", "small", "root", "dve", "act", *[f"slot{j}" for j in range(SLOTS)],
                   *pairs("cut", "hi", "mid", "split"),
                   credited=[f"free{j}" for j in range(SLOTS)] + [f"out{c}" for c in range(HC)]
                   + pairs("made", "rest")) as (block, s):

            def cols(i, u):
                b0, nb = PARTS[u]
                return bass.ds(i * SLAB + b0 * P, nb * P)

            @block.sync
            def _(e):
                with nc.allow_non_contiguous_dma(reason="vectors of 128 words, one to a partition"):
                    for tile, source in load:
                        e.dma_start(tile, source).then_inc(s["small"], 16)
                self.stream_counts(e, s)
                if load:
                    e.wait_ge(s["small"], 16 * len(load))

            @block.gpsimd
            def _(e):
                with e.Fori(0, NSLAB) as i:
                    for u in (0, 1):
                        wait(e, s, f"made{u}", i)
                        e.tensor_copy(self.part[u][:, :], self.hT[:, cols(i, u)]).then_inc(s[f"cut{u}"], 1)

            @block.tensor
            def _(e):
                def product(i, u):
                    wait(e, s, f"cut{u}", i + 1)
                    if u == 0:
                        wait(e, s, "rest1", i)
                    else:
                        wait(e, s, "rest0", i + 1)
                    for b in range(PARTS[u][1]):
                        o = ps[:, SPARE, b * P:(b + 1) * P]
                        piece = self.part[u][:, b * P:(b + 1) * P]
                        if w is None:
                            ins = e.transpose(o, piece, self.ident[:, :])
                        else:
                            ins = e.matmul(o, piece, w, start=True, stop=True)
                    ins.then_inc(s[f"made{u}"], 1)

                def turn(t, kk, next_slab=None, fresh=False):
                    for j in range(SLOTS):
                        for u, (b0, _) in enumerate(PARTS):
                            if fresh and j == b0:
                                wait(e, s, f"split{u}", kk + 1)
                        wait(e, s, f"slot{j}", t * 16 + 16)
                        for part in range(3):
                            for c in range(HC):
                                ins = e.matmul(ps[:, c, 0:CW], self.h3[:, part, bass.ds(kk * SLAB + j * P, P)],
                                               self.ring[:, j, c * CW:(c + 1) * CW], start=False, stop=True,
                                               skip_group_check=True)
                        ins.then_inc(s[f"free{j}"], 1)
                        if next_slab is not None and j in (0, 3):
                            product(next_slab, int(j == 3))

                def clear(half):
                    for c in range(HC):
                        wait(e, s, f"out{c}", half)
                        e.matmul(ps[:, c, 0:CW], self.zero[:, 0:P], self.zero[:, :], start=True, stop=True)

                if w is not None and load:
                    e.wait_ge(s["small"], 16 * len(load))
                product(0, 0)
                product(0, 1)
                clear(0)
                with e.Fori(0, turns - 1) as kk:
                    turn(kk, kk, next_slab=kk + 1, fresh=True)
                turn(turns - 1, turns - 1, fresh=True)
                clear(1)
                with e.Fori(0, turns) as kk:
                    turn(kk + turns, kk)

            def take(c, half):
                o = bass.ds(half * HALF + c * CW, CW)
                return o, self.aggT[:, o]

            @block.scalar
            def _(e):
                if prepare_act is not None:
                    e.wait_ge(s["small"], 16 * len(load))
                    prepare_act(e, s["root"])
                ch = Chain(e, s["act"])
                with e.Fori(0, NSLAB) as i:
                    for u, (_, nb) in enumerate(PARTS):
                        wait(e, s, f"made{u}", i + 1)
                        ch.add(e.copy(self.h3[:, 0, cols(i, u)], ps[:, SPARE, 0:nb * P]))
                        ch.sync()
                        e.sem_inc(s[f"hi{u}"])
                        wait(e, s, f"rest{u}", i + 1)
                        ch.add(e.copy(self.h3[:, 1, cols(i, u)], self.rest[u][:, :]))
                        ch.sync()
                        e.sem_inc(s[f"mid{u}"])
                    ch.restart()
                if not add_self:
                    with e.Fori(0, 2) as half:
                        wait(e, s, f"free{SLOTS - 1}", half * turns + turns)
                        for c in range(1, HC, 2):
                            o, agg = take(c, half)
                            e.copy(agg, ps[:, c, 0:CW]).then_inc(s[f"out{c}"], 1)

            @block.vector
            def _(e):
                ch = Chain(e, s["dve"])
                with e.Fori(0, NSLAB) as i:
                    for u, (b0, nb) in enumerate(PARTS):
                        wait(e, s, f"hi{u}", i + 1)
                        ch.add(e.tensor_tensor(self.rest[u][:, :], ps[:, SPARE, 0:nb * P], self.h3[:, 0, cols(i, u)],
                                               ALU.subtract))
                        ch.sync()
                        e.sem_inc(s[f"rest{u}"])
                        wait(e, s, f"mid{u}", i + 1)
                        ch.add(e.tensor_tensor(self.h3[:, 2, cols(i, u)], self.rest[u][:, :], self.h3[:, 1, cols(i, u)],
                                               ALU.subtract))
                        ch.sync()
                        e.sem_inc(s[f"split{u}"])
                    ch.restart()
                if prepare_dve is not None:
                    e.wait_ge(s["root"], 1)
                    prepare_dve(ch)
                with e.Fori(0, 2) as half:
                    wait(e, s, f"free{SLOTS - 1}", half * turns + turns)
                    for c in range(HC):
                        o, agg = take(c, half)
                        if add_self:
                            e.tensor_tensor(agg, ps[:, c, 0:CW], self.hT[:, o], ALU.add).then_inc(s[f"out{c}"], 1)
                        elif c % 2 == 0:
                            e.tensor_copy(agg, ps[:, c, 0:CW]).then_inc(s[f"out{c}"], 1)


    def dense(self, source, layers, target, first_relu=False):
        nc, ps = self.nc, self.ps
        L = len(layers)
        credited = pairs(*[f"mm{n}_" for n in range(L)], *[f"act{n}_" for n in range(1, L + 1)])
        with stage(nc, "passed", "act", *pairs("act0_"), credited=credited) as (block, s):
            mid = [[self.room(2 * n + u) for u in (0, 1)] for n in range(L)]

            def cols(i, u):
                return bass.ds(i * (2 * CW) + u * CW, CW)

            @block.tensor
            def _(e):
                with e.Fori(0, NCH // 2) as i:
                    for n, (w, _, _, _) in enumerate(layers):
                        for u in (0, 1):
                            if n > 0 or first_relu:
                                wait(e, s, f"act{n}_{u}", i + 1)
                            wait(e, s, f"act{n + 1}_{u}", i)
                            rhs = mid[n][u][:, :] if n > 0 or first_relu else source[:, cols(i, u)]
                            e.matmul(ps[:, 2 * n + u, 0:CW], w, rhs, start=True, stop=True).then_inc(s[f"mm{n}_{u}"], 1)

            @block.scalar
            def _(e):
                ch = Chain(e, s["act"])
                with e.Fori(0, NCH // 2) as i:
                    if first_relu:
                        for u in (0, 1):
                            wait(e, s, f"mm0_{u}", i)
                            ch.add(e.activation(mid[0][u][:, :], source[:, cols(i, u)], ACT.Relu))
                            ch.sync()
                            e.sem_inc(s[f"act0_{u}"])
                    for n, (_, func, scale, bias) in enumerate(layers):
                        for u in (0, 1):
                            wait(e, s, f"mm{n}_{u}", i + 1)
                            if n + 1 < L:
                                wait(e, s, f"mm{n + 1}_{u}", i)
                            out = mid[n + 1][u][:, :] if n + 1 < L else target[:, cols(i, u)]
                            ch.add(e.activation(out, ps[:, 2 * n + u, 0:CW], func, scale=scale, bias=bias))
                            ch.sync()
                            e.sem_inc(s[f"act{n + 1}_{u}"])
                    ch.restart()

    def gru(self, w_in, w_state, b_in, b_state, b_sum):
        nc, ps = self.nc, self.ps
        with stage(nc, "passed", "dve", "act", *pairs("mm", "rz", "new"), credited=pairs("pre", "next")) as (block, s):
            r, z, pre, new = [[self.room(2 * n + u) for u in (0, 1)] for n in range(4)]

            def cols(i, u):
                return bass.ds(i * (2 * CW) + u * CW, CW)

            @block.tensor
            def _(e):
                with e.Fori(0, NCH // 2) as i:
                    for u in (0, 1):
                        wait(e, s, f"pre{u}", i)
                        c, b = cols(i, u), 4 * u
                        for g in (0, 1):
                            e.matmul(ps[:, b + g, 0:CW], w_in[g], self.aggT[:, c], start=True, stop=False)
                            e.matmul(ps[:, b + g, 0:CW], w_state[g], self.hT[:, c], start=False, stop=True)
                        e.matmul(ps[:, b + 3, 0:CW], w_state[2], self.hT[:, c], start=True, stop=True)
                        e.matmul(ps[:, b + 2, 0:CW], w_in[2], self.aggT[:, c], start=True, stop=True)\
                            .then_inc(s[f"mm{u}"], 1)

            @block.scalar
            def _(e):
                ch = Chain(e, s["act"])
                with e.Fori(0, NCH // 2) as i:
                    for u in (0, 1):
                        wait(e, s, f"mm{u}", i + 1)
                        wait(e, s, f"next{u}", i)
                        ch.add(e.activation(r[u][:, :], ps[:, 4 * u, 0:CW], ACT.Sigmoid, bias=b_sum[0]))
                        ch.add(e.activation(z[u][:, :], ps[:, 4 * u + 1, 0:CW], ACT.Sigmoid, bias=b_sum[1]))
                        ch.sync()
                        e.sem_inc(s[f"rz{u}"])
                    for u in (0, 1):
                        wait(e, s, f"pre{u}", i + 1)
                        ch.add(e.activation(new[u][:, :], pre[u][:, :], ACT.Tanh, bias=b_in[2]))
                        ch.sync()
                        e.sem_inc(s[f"new{u}"])
                    ch.restart()

            @block.vector
            def _(e):
                ch = Chain(e, s["dve"])
                with e.Fori(0, NCH // 2) as i:
                    for u in (0, 1):
                        wait(e, s, f"rz{u}", i + 1)
                        ch.add(e.scalar_tensor_tensor(pre[u][:, :], ps[:, 4 * u + 3, 0:CW], b_state[2], r[u][:, :],
                                                      ALU.add, ALU.mult))
                        ch.sync()
                        ch.add(e.tensor_tensor(pre[u][:, :], ps[:, 4 * u + 2, 0:CW], pre[u][:, :], ALU.add))
                        ch.sync()
                        e.sem_inc(s[f"pre{u}"])
                    for u in (0, 1):
                        c = cols(i, u)
                        wait(e, s, f"new{u}", i + 1)
                        ch.add(e.tensor_tensor(self.hT[:, c], self.hT[:, c], new[u][:, :], ALU.subtract))
                        ch.sync()
                        ch.add(e.tensor_tensor(self.hT[:, c], self.hT[:, c], z[u][:, :], ALU.mult))
                        ch.sync()
                        ch.add(e.tensor_tensor(self.hT[:, c], self.hT[:, c], new[u][:, :], ALU.add))
                        ch.sync()
                        e.sem_inc(s[f"next{u}"])
                    ch.restart()


    def target_scores(self, w_rep, scores):
        nc, ps = self.nc, self.ps
        with stage(nc, "passed", *pairs("mm"), credited=pairs("out")) as (block, s):
            def cols(i, u):
                return bass.ds(i * (2 * CW) + u * CW, CW)

            @block.tensor
            def _(e):
                with e.Fori(0, NCH // 2) as i:
                    for u in (0, 1):
                        wait(e, s, f"out{u}", i)
                        e.matmul(ps[:, u, 0:CW], w_rep, self.hT[:, cols(i, u)], start=True, stop=True)\
                            .then_inc(s[f"mm{u}"], 1)

            @block.vector
            def _(e):
                with e.Fori(0, NCH // 2) as i:
                    for u in (0, 1):
                        wait(e, s, f"mm{u}", i + 1)
                        e.tensor_copy(scores[:, cols(i, u)], ps[:, u, 0:CW]).then_inc(s[f"out{u}"], 1)

    def attend(self, scores, source_scores, gate_room):
        nc, ps = self.nc, self.ps
        turns = NB // SLOTS
        R = 3
        names = ["passed"] + [f"{n}{j}" for n in ("cut", "slot") for j in range(SLOTS)]\
            + [f"{n}{c}" for n in ("gate", "weighed") for c in range(HC)]
        credited = [f"{n}{j}" for n in ("free", "used_cut") for j in range(SLOTS)] + [f"{n}{c}" for n in ("out", "used") for c in range(HC)]
        with ExitStack() as tmp, stage(nc, *names, credited=credited) as (block, s):
            gate = gate_room.rearrange("p (c t) -> p c t", t=CW)
            piece = scratch(nc, tmp, "piece", [P, SLOTS, P])

            @block.sync
            def _(e):
                self.stream_counts(e, s)

            @block.gpsimd
            def _(e):
                with e.Fori(0, 2) as half:
                    with e.Fori(0, turns) as kk:
                        for j in range(SLOTS):
                            wait(e, s, f"used_cut{j}", half * turns + kk)
                            e.tensor_copy(piece[:, j, :], self.msg[:, bass.ds(kk * (SLOTS * P) + j * P, P)])\
                                .then_inc(s[f"cut{j}"], 1)

            @block.scalar
            def _(e):
                with e.Fori(0, 2) as half:
                    with e.Fori(0, turns) as kk:
                        for j in range(SLOTS):
                            n = half * NB + kk * SLOTS + j
                            for c in range(HC):
                                wait(e, s, f"used{c}", n)
                                e.activation(gate[:, c, :], scores[:, bass.ds(half * HALF + c * CW, CW)], ACT.Sigmoid,
                                             bias=source_scores[:, bass.ds(kk * SLOTS + j, 1)])\
                                    .then_inc(s[f"gate{c}"], 1)

            @block.vector
            def _(e):
                with e.Fori(0, 2) as half:
                    with e.Fori(0, turns) as kk:
                        for j in range(SLOTS):
                            n = half * NB + kk * SLOTS + j
                            wait(e, s, f"slot{j}", half * (16 * turns) + kk * 16 + 16)
                            for c in range(HC):
                                wait(e, s, f"gate{c}", n + 1)
                                ins = e.tensor_tensor(gate[:, c, :], gate[:, c, :], self.ring[:, j, c * CW:(c + 1) * CW],
                                                      ALU.mult).then_inc(s[f"weighed{c}"], 1)
                            wait(e, s, f"weighed{HC - 1}", n + 1)
                            e.sem_inc(s[f"free{j}"])
                    wait(e, s, f"used{HC - 1}", half * NB + NB)
                    for c in range(HC):
                        e.tensor_copy(self.aggT[:, bass.ds(half * HALF + c * CW, CW)], ps[:, c, 0:CW])\
                            .then_inc(s[f"out{c}"], 1)

            @block.tensor
            def _(e):
                with e.Fori(0, 2) as half:
                    for c in range(HC):
                        wait(e, s, f"out{c}", half)
                        e.matmul(ps[:, c, 0:CW], self.zero[:, 0:P], self.zero[:, :], start=True, stop=True)
                    with e.Fori(0, turns) as kk:
                        for j in range(SLOTS):
                            n = half * NB + kk * SLOTS + j
                            wait(e, s, f"cut{j}", half * turns + kk + 1)
                            for c in range(HC):
                                wait(e, s, f"weighed{c}", n + 1)
                                ins = e.matmul(ps[:, c, 0:CW], piece[:, j, :], gate[:, c, :], start=False, stop=True,
                                               skip_group_check=True)
                                ins.then_inc(s[f"used{c}"], 1)
                        wait(e, s, f"used{HC - 1}", half * NB + kk * SLOTS + SLOTS)
                        for j in range(SLOTS):
                            e.sem_inc(s[f"used_cut{j}"])

    def batch_norm(self, gamma, beta):
        nc = self.nc
        W = 250
        assert N % W == 0
        with ExitStack() as tmp, stage(nc, "passed", "dve", "stats", "root", "inv", "done") as (block, s):
            def sb(n, shape):
                return scratch(nc, tmp, n, shape)
            stats, mv = sb("bn_st", [P, (N // W) * 6]), sb("bn_mv", [P, 2])
            root, inv, t, scale, shift = (sb(f"bn_{n}", [P, 1]) for n in ("root", "inv", "t", "scale", "shift"))

            @block.vector
            def _(e):
                ch = Chain(e, s["dve"])
                with e.Fori(0, N // W) as i:
                    e.bn_stats(stats[:, bass.ds(i * 6, 6)], self.hT[:, bass.ds(i * W, W)]).then_inc(s["stats"], 1)
                wait(e, s, "stats", N // W)
                ch.add(e.bn_aggr(mv[:, :], stats[:, :])); ch.sync()
                e.sem_inc(s["stats"])
                wait(e, s, "root", 1)
                self.rsqrt(ch, inv[:, :], mv[:, 1:2], root[:, :], t[:, :])
                ch.add(e.tensor_tensor(scale[:, :], gamma, inv[:, :], ALU.mult)); ch.sync()
                ch.add(e.scalar_tensor_tensor(shift[:, :], mv[:, 0:1], -1.0, scale[:, :], ALU.mult, ALU.mult)); ch.sync()
                ch.add(e.tensor_tensor(shift[:, :], shift[:, :], beta, ALU.add)); ch.sync()
                e.sem_inc(s["inv"])

            @block.scalar
            def _(e):
                wait(e, s, "stats", N // W + 1)
                e.activation(root[:, :], mv[:, 1:2], ACT.Sqrt, bias=self.eps[:, 0:1]).then_inc(s["root"], 1)
                wait(e, s, "inv", 1)
                with e.Fori(0, NSLAB) as i:
                    e.activation(self.hT[:, bass.ds(i * SLAB, SLAB)], self.hT[:, bass.ds(i * SLAB, SLAB)], ACT.Identity,
                                 scale=scale[:, 0:1], bias=shift[:, 0:1]).then_inc(s["done"], 1)
                wait(e, s, "done", NSLAB)


    def finish(self, out):
        nc, ps = self.nc, self.ps
        full = (N // P) * P
        with stage(nc, "passed", "store", *pairs("cut"), credited=pairs("turned", "added")) as (block, s):
            def cols(i, u):
                b0, nb = PARTS[u]
                return bass.ds(i * SLAB + b0 * P, nb * P)

            @block.gpsimd
            def _(e):
                with e.Fori(0, NSLAB) as i:
                    for u in (0, 1):
                        wait(e, s, f"turned{u}", i)
                        e.tensor_copy(self.part[u][:, :], self.hT[:, cols(i, u)]).then_inc(s[f"cut{u}"], 1)

            @block.tensor
            def _(e):
                with e.Fori(0, NSLAB) as i:
                    for u, (_, nb) in enumerate(PARTS):
                        wait(e, s, f"cut{u}", i + 1)
                        wait(e, s, f"added{u}", i)
                        for b in range(nb):
                            ins = e.transpose(ps[:, u, b * P:(b + 1) * P], self.part[u][:, b * P:(b + 1) * P],
                                              self.ident[:, :])
                        ins.then_inc(s[f"turned{u}"], 1)

            @block.vector
            def _(e):
                with e.Fori(0, NSLAB) as i:
                    for u, (b0, nb) in enumerate(PARTS):
                        wait(e, s, f"turned{u}", i + 1)
                        e.tensor_tensor(self.xN[:, cols(i, u)], ps[:, u, 0:nb * P], self.xN[:, cols(i, u)], ALU.add)\
                            .then_inc(s[f"added{u}"], 1)

            @block.sync
            def _(e):
                with e.Fori(0, NSLAB - 1) as i:
                    for u in (0, 1):
                        wait(e, s, f"added{u}", i + 1)
                    e.dma_start(out[bass.ds(i * SLAB, SLAB), :].rearrange("(k p) f -> p k f", p=P),
                                self.xN[:, bass.ds(i * SLAB, SLAB)].rearrange("p (k f) -> p k f", f=D))\
                        .then_inc(s["store"], 16)
                last = (NSLAB - 1) * SLAB
                for u in (0, 1):
                    wait(e, s, f"added{u}", NSLAB)
                e.dma_start(out[last:full, :].rearrange("(k p) f -> p k f", p=P),
                            self.xN[:, last:full].rearrange("p (k f) -> p k f", f=D)).then_inc(s["store"], 16)
                e.dma_start(out[full:N, :], self.xN[0:N - full, full:NP]).then_inc(s["store"], 16)
                wait(e, s, "store", 16 * (NSLAB + 1))


def program(nc, a, out):
    count = nc.dram_tensor("count", [(NP + 1) * PITCH, 1], F16, kind="Internal").ap()
    build_counts(nc, a["src"], a["dst"], count)

    with ExitStack() as ctx:
        net = Net(nc, ctx, count)
        sb = net.sb

        def gates(m):
            return [m[g * D:(g + 1) * D, :] for g in range(3)]

        names, matrices = {}, []
        for key, blocks in (("1ih", gates(a["L1_gnn_W_ih"])), ("1hh", gates(a["L1_gnn_W_hh"])),
                            ("2e1", [a["L2_gnn_enc_w1"]]), ("2e2", [a["L2_gnn_enc_w2"]]),
                            ("2ih", gates(a["L2_gnn_gru_wih"])), ("2hh", gates(a["L2_gnn_gru_whh"])),
                            ("2d1", [a["L2_gnn_dec_w1"]]), ("2d2", [a["L2_gnn_dec_w2"]]), ("3", [a["L3_gnn_W"]])):
            names[key] = range(len(matrices), len(matrices) + len(blocks))
            matrices += blocks

        def column(v):
            return v.rearrange("(p o) -> p o", o=1)

        def three(v):
            return v.rearrange("(g p) -> p g", p=P)

        b1i, b1h, b1s = sb("b1i", [P, 3]), sb("b1h", [P, 3]), sb("b1s", [P, 3])
        b2i, b2h, b2s = sb("b2i", [P, 3]), sb("b2h", [P, 3]), sb("b2s", [P, 3])
        gam, bet, e1, e2, d1, d2, b3 = (sb(n, [P, 1]) for n in ("gam", "bet", "e1", "e2", "d1", "d2", "b3"))
        w_att = sb("w_att", [P, 2])
        b_att = sb("b_att", [P, 1])
        b_msg = sb("b_msg", [P, D])
        w_msg = sb("w_msg", [P, D])
        att_rep = sb("att_rep", [P, P])
        vectors = [(b1i[:, :], three(a["L1_gnn_b_ih"])), (b1h[:, :], three(a["L1_gnn_b_hh"])),
                   (b2i[:, :], three(a["L2_gnn_gru_bih"])), (b2h[:, :], three(a["L2_gnn_gru_bhh"])),
                   (gam[:, :], column(a["L1_gnn_gamma"])), (bet[:, :], column(a["L1_gnn_beta"])),
                   (e1[:, :], column(a["L2_gnn_enc_b1"])), (e2[:, :], column(a["L2_gnn_enc_b2"])),
                   (d1[:, :], column(a["L2_gnn_dec_b1"])), (d2[:, :], column(a["L2_gnn_dec_b2"])),
                   (b3[:, :], column(a["L3_gnn_b"])),
                   (w_att[:, :], a["L1_gnn_W_att"].rearrange("(g p) o -> p (g o)", p=P)),
                   (b_att[:, :], a["L1_gnn_b_att"].rearrange("(a o) -> a o", a=1).to_broadcast([P, 1]))]
        directs = [(b_msg[:, :], a["L1_gnn_b_msg"].rearrange("(a f) -> a f", a=1).to_broadcast([P, D])),
                   (w_msg[:, :], a["L1_gnn_W_msg"])]
        net.setup(a["x"], matrices, vectors, directs)

        def wt(key):
            return [net.wT[:, i, :] for i in names[key]]

        with stage(nc, "one") as (block, s):
            @block.vector
            def _(e):
                e.tensor_tensor(b1s[:, :], b1i[:, :], b1h[:, :], ALU.add).then_inc(s["one"], 1)
                e.tensor_tensor(b2s[:, :], b2i[:, :], b2h[:, :], ALU.add).then_inc(s["one"], 1)
                e.tensor_copy(att_rep[:, :], w_att[:, 1:2].to_broadcast([P, P])).then_inc(s["one"], 1)
                wait(e, s, "one", 3)

        net.norm(add=False)
        w12 = sb("w12", [P, 2, D])
        vec = sb("vec", [P, 5, 2])
        bn = sb("bn", [P, 4, 2])
        layers0 = 3
        with nc.Fori(0, layers0) as layer:
            load = [(w12[:, n, :], m.rearrange("l i o -> (l i) o")[bass.ds(layer * D, D), :])
                    for n, m in enumerate((a["L0_gnn_W1"], a["L0_gnn_W2"]))]
            load += [(vec[:, 0, n:n + 1], v.rearrange("l (f o) -> (l f) o", o=1)[bass.ds(layer * D, D), :])
                     for n, v in enumerate((a["L0_gnn_b1"], a["L0_gnn_b2"]))]
            load += [(vec[:, 1 + q, n:n + 1],
                      v.rearrange("l n (f o) -> (l n f) o", o=1)[bass.ds(layer * (2 * D) + n * D, D), :])
                     for q, v in enumerate((a["L0_gnn_g"], a["L0_gnn_be"], a["L0_gnn_rm"], a["L0_gnn_rv"]))
                     for n in (0, 1)]

            def norm_roots(e, done):
                e.activation(bn[:, 0, :], vec[:, 4, :], ACT.Sqrt, bias=net.eps[:, 0:1]).then_inc(done, 1)

            def norm_factors(ch):
                e = ch.engine
                net.rsqrt(ch, bn[:, 1, :], vec[:, 4, :], bn[:, 0, :], bn[:, 2, :])
                ch.add(e.tensor_tensor(bn[:, 1, :], bn[:, 1, :], vec[:, 1, :], ALU.mult)); ch.sync()
                ch.add(e.tensor_tensor(bn[:, 3, :], vec[:, 0, :], vec[:, 3, :], ALU.subtract)); ch.sync()
                ch.add(e.tensor_tensor(bn[:, 3, :], bn[:, 3, :], bn[:, 1, :], ALU.mult)); ch.sync()
                ch.add(e.tensor_tensor(bn[:, 3, :], bn[:, 3, :], vec[:, 2, :], ALU.add)); ch.sync()

            net.aggregate(add_self=True, load=load, prepare_act=norm_roots, prepare_dve=norm_factors)
            net.dense(net.aggT, [(w12[:, n, :], ACT.Relu, bn[:, 1, n:n + 1], bn[:, 3, n:n + 1]) for n in (0, 1)], net.hT)

        net.norm(add=True)
        source_scores = sb("source_scores", [P, NB])
        scores = net.h3[:, 0:2, :].rearrange("p a t -> p (a t)").bitcast(F32)
        net.messages(w_msg[:, :], b_msg[:, :], w_att[:, 0:1], b_att[:, 0:1], source_scores)
        net.target_scores(att_rep[:, :], scores)
        net.attend(scores, source_scores, net.h3[:, 2, :].bitcast(F32))
        net.gru(wt("1ih"), wt("1hh"), [b1i[:, g:g + 1] for g in range(3)], [b1h[:, g:g + 1] for g in range(3)],
                [b1s[:, g:g + 1] for g in range(3)])
        net.batch_norm(gam[:, :], bet[:, :])

        net.norm(add=True)
        net.dense(net.hT, [(wt("2e1")[0], ACT.Relu, 1.0, e1[:, :]), (wt("2e2")[0], ACT.Identity, 1.0, e2[:, :])], net.hT)
        w_step = sb("w_step", [P, D])
        steps = 5
        with nc.Fori(0, steps) as step:
            net.aggregate(w_step[:, :], load=[(w_step[:, :], a["L2_gnn_conv_w"].rearrange("l i o -> (l i) o")
                                               [bass.ds(step * D, D), :])])
            net.gru(wt("2ih"), wt("2hh"), [b2i[:, g:g + 1] for g in range(3)], [b2h[:, g:g + 1] for g in range(3)],
                    [b2s[:, g:g + 1] for g in range(3)])
        net.dense(net.hT, [(wt("2d1")[0], ACT.Relu, 1.0, d1[:, :]), (wt("2d2")[0], ACT.Sigmoid, 1.0, d2[:, :])], net.hT,
                  first_relu=True)

        net.norm(add=True)
        net.aggregate()
        net.dense(net.aggT, [(wt("3")[0], ACT.Identity, 1.0, b3[:, :])], net.hT)
        net.finish(out)


def kernel(**inputs):
    import concourse.bacc as bacc
    from concourse.bass_utils import run_bass_kernel_spmd

    nc = bacc.Bacc("TRN2", target_bir_lowering=False, num_devices=1)
    arrays, aps = {}, {}
    for name, value in inputs.items():
        value = np.ascontiguousarray(value)
        arrays[f"in_{name}"] = value
        aps[name] = nc.dram_tensor(f"in_{name}", value.shape, mybir.dt.from_np(value.dtype), kind="ExternalInput").ap()
    out = nc.dram_tensor("out", (N, D), F32, kind="ExternalOutput").ap()
    program(nc, aps, out)
    result = run_bass_kernel_spmd(nc, [arrays], core_ids=[0])
    return np.asarray(result.results[0]["out"])
```

```python
from contextlib import ExitStack, contextmanager

import numpy as np

import concourse.bass as bass
from concourse import mybir

F32 = mybir.dt.float32
BF16 = mybir.dt.bfloat16
F16 = mybir.dt.float16
F32R = mybir.dt.float32r
I32 = mybir.dt.int32
U32 = mybir.dt.uint32
ALU = mybir.AluOpType
ACT = mybir.ActivationFunctionType

N = 6250
E = 100000
D = 128
P = 128
NB = -(-N // P)
NP = NB * P
SLAB_BLOCKS = 7
NSLAB = NB // SLAB_BLOCKS
SLAB = SLAB_BLOCKS * P
CW = 448
NCH = NP // CW
HC = NCH // 2
HALF = HC * CW
SLOTS = 7
LN_EPS = 1e-5
HIGH_BITS = -(1 << 12)
WIDENERS = [("scalar", 0, 3), ("vector", 3, 2), ("vector", 5, 2)]
assert NB % SLAB_BLOCKS == 0 and NP % CW == 0 and NCH % 2 == 0 and SLAB == 2 * CW and NB % SLOTS == 0

PARTS = [(0, 4), (4, 3)]

SRC_SHIFT = 13
PITCH = 1 << SRC_SHIFT
KEY_BASE = 0x20000000
KEY_MASK = KEY_BASE - 1
GROUP = 8
TROWS = 112
TCH = 7
NT = TROWS * TCH
NG = NT // GROUP
GW = GROUP * P
FULL_T, TAIL = divmod(E, P)
assert NT * P >= E and NP <= PITCH and NG % 2 == 0
FIRST_MARK = 2048
EXACT = 2048
MOST = 61440
PLANES = 3
PLANE_ROWS = NP + 1
AT_ONCE = 4
AHEAD = 18
PAD_TARGET = 1024


class Semaphores(dict):
    credited = frozenset()


@contextmanager
def stage(nc, *names, credited=()):
    s = Semaphores((n, nc.alloc_semaphore(f"{n}_{nc.next_id()}")) for n in (*names, *credited))
    s.credited = frozenset(credited)
    for name in credited:
        nc.gpsimd.sem_inc(s[name])
    if credited:
        nc.all_engine_barrier()
    with nc.Block() as block:
        yield block, s
    nc.clear_and_free_semaphores(list(s.values()))
    nc.all_engine_barrier()


def pairs(*names):
    return [f"{n}{u}" for n in names for u in (0, 1)]


def wait(engine, s, name, value):
    engine.wait_ge(s[name], value + (name in s.credited))
    if not isinstance(value, int):
        engine.sem_inc(s["passed"])


def scratch(nc, ctx, name, shape, dt=F32):
    return ctx.enter_context(nc.sbuf_tensor(f"{name}_{nc.next_id()}", shape, dt))


class Chain:

    def __init__(self, engine, sem):
        self.engine, self.sem, self.n = engine, sem, 0

    def add(self, instruction):
        instruction.then_inc(self.sem, 1)
        self.n += 1
        return instruction

    def sync(self):
        self.engine.wait_ge(self.sem, self.n)

    def restart(self):
        self.sync()
        self.engine.sem_clear(self.sem)
        self.n = 0


def build_counts(nc, src, dst, count, more, many, ps, meanwhile):
    keyrow = nc.dram_tensor("keyrow", [NT * P], F32, kind="Internal").ap()
    with ExitStack() as ctx:
        def sb(name, shape, dt):
            return ctx.enter_context(nc.sbuf_tensor(name, shape, dt))

        ident = sb("b_ident", [P, P], F32)
        s_rows = sb("s_rows", [TROWS, TCH, P], I32)
        d_rows = sb("d_rows", [TROWS, TCH, P], I32)
        key_rows = sb("key_rows", [TROWS, TCH, P], I32)
        keyT = sb("keyT", [P, NT], F32)
        low_rows = sb("low_rows", [TROWS, TCH * P], I32)
        classes = sb("classes", [TROWS, TCH * P], BF16)
        ones_sq = sb("ones_sq", [TROWS, P], F32)
        class_i = sb("class_i", [P, P], I32)
        class_no = sb("class_no", [P, P], F32)
        part_hist = sb("part_hist", [TROWS, P], F32)
        largest = sb("largest", [P, 1], F32)
        zeros = sb("zeros", [P, NP], F16)
        weight = sb("weight", [P, GROUP, GW], F32)
        dump_i = sb("dump_i", [P, GROUP], I32)
        dump = sb("dump", [P, GROUP], I32)
        rows = [sb(f"rows{b}", [P, GW], F32) for b in (0, 1)]
        junk = sb("junk", [P, GROUP, GW], BF16)
        acc = sb("acc", [P, GROUP], F32)
        repeated = sb("repeated", [P, GROUP], U32)
        where = sb("where", [P, GROUP], I32)
        index = [sb(f"index{b}", [P, GROUP], U32) for b in (0, 1)]
        amount = [sb(f"amount{b}", [P, GROUP], F16) for b in (0, 1)]
        amount_f32 = [sb(f"amount_f32_{b}", [P, GROUP], F32) for b in (0, 1)]
        zeroed = nc.alloc_semaphore("zeroed")

        def filler(table):
            parts = mybir.dt.size(table.dtype) // 2
            dmas = NB * parts + 1

            def fill(e, sem, blocks=(0, NB)):
                zero = zeros[:, :].bitcast(table.dtype)
                if blocks[0] == 0:
                    e.dma_start(table[NP:NP + 1, :].rearrange("a (p t) -> (a p) t", p=16), zero[0:16, 0:PITCH // 16])\
                        .then_inc(sem, 16)
                with e.Fori(*blocks) as k:
                    for h in range(parts):
                        e.dma_start(table[bass.ds(k * P, P), h * (NP // parts):(h + 1) * (NP // parts)],
                                    zero[:, 0:NP // parts]).then_inc(sem, 16)
            return fill, dmas

        first = count.rearrange("(s t) o -> s (t o)", t=PITCH)

        before_copies = []
        with ExitStack() as tmp, stage(nc, "pad", "edges", "id0", "id1", "ord", "zeros", "dve", "keys", "tr", "kout")\
                as (block, s):
            order_i = scratch(nc, tmp, "order_i", [P, GROUP, GW], I32)
            whole = (TCH - 1) * TROWS

            @block.gpsimd
            def _(e):
                e.memset(ident[:, :], 0.0).then_inc(s["id0"], 1)
                wait(e, s, "id0", 1)
                e.affine_select(out=ident[:, :], in_=ident[:, :], compare_op=ALU.not_equal, fill=1.0, base=0,
                                pattern=[[-1, P]], channel_multiplier=1).then_inc(s["id1"], 1)
                e.iota(order_i[:, :, :], pattern=[[P, GROUP], [-1, GW]], base=0, channel_multiplier=1)\
                    .then_inc(s["ord"], 1)
                e.iota(dump_i[:, :], pattern=[[P, GROUP]], base=NP << SRC_SHIFT, channel_multiplier=1)\
                    .then_inc(s["ord"], 1)
                e.iota(class_i[:, :], pattern=[[1, P]], base=0, channel_multiplier=0).then_inc(s["ord"], 1)

            @block.sync
            def _(e):
                for n, (edges, tile) in enumerate(((src, s_rows), (dst, d_rows))):
                    e.dma_start(tile[:, 0:TCH - 1, :], edges[0:whole * P].rearrange("(c p l) -> p c l", p=TROWS, l=P))\
                        .then_inc(s["edges"], 16)
                    wait(e, s, "pad", 2 * n + 2)
                    e.dma_start(tile[0:FULL_T - whole, TCH - 1, :],
                                edges[whole * P:FULL_T * P].rearrange("(p l) -> p l", l=P)).then_inc(s["edges"], 16)
                    e.dma_start(tile[FULL_T - whole:FULL_T - whole + 1, TCH - 1, 0:TAIL],
                                edges[FULL_T * P:E].rearrange("(a l) -> a l", a=1)).then_inc(s["edges"], 16)
                wait(e, s, "zeros", 1)
                filler(first)[0](e, zeroed, (0, AT_ONCE))
                wait(e, s, "keys", 1)
                e.dma_start(keyrow.rearrange("(c p l) -> p c l", p=TROWS, l=P), key_rows[:, :, :].bitcast(F32))\
                    .then_inc(s["kout"], 16)
                wait(e, s, "kout", 16)
                filler(first)[0](e, zeroed, (AT_ONCE, AHEAD))

            @block.vector
            def _(e):
                ch = Chain(e, s["dve"])
                for tile, value in ((s_rows, NP), (d_rows, PAD_TARGET)):
                    e.memset(tile[:, TCH - 1, :], value).then_inc(s["pad"], 2)
                e.memset(zeros[:, :], 0.0).then_inc(s["zeros"], 1)
                ch.add(e.memset(ones_sq[:, :], 1.0))
                wait(e, s, "ord", 3)
                ch.add(e.tensor_copy(class_no[:, :], class_i[:, :]))
                ch.add(e.tensor_scalar(weight[:, :, :], order_i[:, :, :], 0.0, float(FIRST_MARK), ALU.is_gt, ALU.mult))
                ch.add(e.tensor_scalar(dump[:, :], dump_i[:, :], KEY_BASE, None, ALU.bitwise_or))
                ch.sync()
                ch.add(e.tensor_scalar(weight[:, :, :], weight[:, :, :], 1.0, None, ALU.add))
                wait(e, s, "edges", 6 * 16)
                ch.add(e.tensor_scalar(key_rows[:, :, :], s_rows[:, :, :], SRC_SHIFT, KEY_BASE,
                                       ALU.logical_shift_left, ALU.bitwise_or))
                ch.add(e.tensor_scalar(low_rows[:, :], s_rows[:, :, :].rearrange("p c l -> p (c l)"), P - 1, None,
                                       ALU.bitwise_and))
                ch.sync()
                ch.add(e.tensor_copy(classes[:, :], low_rows[:, :]))
                before_copies.append(ch.n)
                e.tensor_tensor(key_rows[:, :, :], key_rows[:, :, :], d_rows[:, :, :], ALU.bitwise_or)\
                    .then_inc(s["keys"], 1)
                for c in range(TCH):
                    wait(e, s, "tr", c + 1)
                    ch.add(e.tensor_copy(keyT[:, c * TROWS:(c + 1) * TROWS], ps[:, c % 2, 0:TROWS]))
                ch.sync()

            @block.tensor
            def _(e):
                wait(e, s, "keys", 1)
                wait(e, s, "id1", 1)
                for c in range(TCH):
                    if c >= 2:
                        wait(e, s, "dve", before_copies[0] + c - 1)
                    e.transpose(ps[:, c % 2, 0:TROWS], key_rows[:, c, :].bitcast(F32), ident[0:TROWS, 0:TROWS])\
                        .then_inc(s["tr"], 1)

        meanwhile()

        def scatter(counts, table, amount, filling=None, histogram=None):
            fill, dmas = filler(table)
            with stage(nc, "zero", "dve", "hist", "total", "landed", "passed", *pairs("load", "made"),
                       credited=pairs("used", "freed")) as (block, s):
                @block.sync
                def _(e):
                    if filling is None:
                        fill(e, s["zero"])
                    else:
                        fill(e, filling, (AHEAD, NB))

                @block.scalar
                def _(e):
                    with e.Fori(0, NG // 2) as i:
                        for b in (0, 1):
                            wait(e, s, f"used{b}", i)
                            e.dma_start(rows[b][:, :], keyrow[bass.ds(i * (2 * GW) + b * GW, GW)]
                                        .rearrange("(a l) -> a l", a=1).to_broadcast([P, GW]))\
                                .then_inc(s[f"load{b}"], 16)
                    wait(e, s, "used0", NG // 2)
                    wait(e, s, "used1", NG // 2)

                @block.vector
                def _(e):
                    ch = Chain(e, s["dve"])
                    if histogram is not None:
                        histogram(ch, s)
                    with e.Fori(0, NG // 2) as i:
                        for b in (0, 1):
                            wait(e, s, f"load{b}", i * 16 + 16)
                            col = i * (2 * GROUP) + b * GROUP
                            for t in range(GROUP):
                                ch.add(e.scalar_tensor_tensor(
                                    junk[:, t, :], rows[b][:, :], keyT[:, bass.ds(col + t, 1)],
                                    weight[:, t, :], ALU.is_equal, ALU.mult, accum_out=acc[:, t:t + 1]))
                            ch.add(e.tensor_copy(where[:, :], keyT[:, bass.ds(col, GROUP)].bitcast(I32)))
                            ch.sync()
                            e.sem_inc(s[f"used{b}"])
                            ch.add(e.tensor_scalar(repeated[:, :], acc[:, :], FIRST_MARK - 0.5, None, ALU.is_gt))
                            ch.sync()
                            ch.add(e.copy_predicated(where[:, :], repeated[:, :], dump[:, :]))
                            ch.sync()
                            wait(e, s, f"freed{b}", i)
                            ch.add(e.scalar_tensor_tensor(amount[b][:, :], acc[:, :], FIRST_MARK - 0.5, acc[:, :],
                                                          ALU.is_lt, ALU.mult))
                            ch.add(e.tensor_scalar(index[b][:, :], where[:, :].bitcast(U32), KEY_MASK, None,
                                                   ALU.bitwise_and))
                            ch.sync()
                            e.sem_inc(s[f"made{b}"])
                        ch.restart()

                if histogram is not None:
                    @block.tensor
                    def _(e):
                        wait(e, s, "hist", 1)
                        e.matmul(ps[:, 0, 0:P], ones_sq[:, :], part_hist[:, :], start=True, stop=True)\
                            .then_inc(s["total"], 1)

                @block.gpsimd
                def _(e):
                    e.wait_ge(filling or s["zero"], 16 * dmas)
                    with e.Fori(0, NG // 2) as i:
                        for b in (0, 1):
                            wait(e, s, f"made{b}", i + 1)
                            for t in range(GROUP):
                                e.indirect_dma_start(
                                    out=counts, out_offset=bass.IndirectOffsetOnAxis(ap=index[b][:, t:t + 1], axis=0),
                                    in_=amount[b][:, t:t + 1], in_offset=None, compute_op=ALU.add)\
                                    .then_inc(s["landed"], 16)
                            wait(e, s, "landed", i * (2 * GROUP * 16) + (b + 1) * GROUP * 16)
                            e.sem_inc(s[f"freed{b}"])

        def find_many(ch, s):
            e = ch.engine
            with e.Fori(0, P // GROUP) as i:
                for t in range(GROUP):
                    ch.add(e.tensor_scalar(
                        junk[0:TROWS, t, 0:TCH * P], classes[:, :], class_no[0:TROWS, bass.ds(i * GROUP + t, 1)],
                        0.0, ALU.is_equal, ALU.add, accum_out=acc[0:TROWS, t:t + 1]))
                ch.sync()
                ch.add(e.tensor_copy(part_hist[:, bass.ds(i * GROUP, GROUP)], acc[0:TROWS, :]))
                ch.restart()
            e.sem_inc(s["hist"])
            e.wait_ge(s["total"], 1)
            ch.add(e.tensor_reduce(largest[:, :], ps[:, 0, 0:P], mybir.AxisListType.X, ALU.max)); ch.sync()
            ch.add(e.tensor_scalar(many, largest[:, :], EXACT - 0.5, None, ALU.is_gt))
            ch.restart()

        scatter(count, first, amount, zeroed, histogram=find_many)
        nc.clear_and_free_semaphores([zeroed])
        nc.all_engine_barrier()
        flag = nc.values_load(many[0:1, 0:1], min_val=0, max_val=1)

        with nc.If(flag > 0):
            exact = nc.dram_tensor("exact", [PLANE_ROWS * PITCH, 1], F32, kind="Internal").ap()
            table = exact.rearrange("(s t) o -> s (t o)", t=PITCH)
            scatter(exact, table, amount_f32)
            wide = [sb(f"wide{u}", [P, HALF // 2], F32) for u in (0, 1)]
            cut = [[sb(f"cut{u}_{p}", [P, HALF // 2], F16) for p in range(PLANES)] for u in (0, 1)]
            with nc.Fori(0, NB) as k:
                with nc.Fori(0, 2) as h:
                    def piece(t, row, u):
                        return t[bass.ds(k * P + row, P), bass.ds(h * HALF + u * (HALF // 2), HALF // 2)]

                    with stage(nc, "dve", "stored", *pairs("load", "cut")) as (block, s):
                        @block.sync
                        def _(e):
                            for u in (0, 1):
                                e.dma_start(wide[u][:, :], piece(table, 0, u)).then_inc(s[f"load{u}"], 16)
                            for u in (0, 1):
                                wait(e, s, f"cut{u}", 1)
                                for p in range(PLANES):
                                    to = piece(first, 0, u) if p == 0 else piece(more, (p - 1) * NP, u)
                                    e.dma_start(to, cut[u][p][:, :])\
                                        .then_inc(s["stored"], 16)
                            wait(e, s, "stored", 2 * PLANES * 16)

                        @block.vector
                        def _(e):
                            ch = Chain(e, s["dve"])
                            for u in (0, 1):
                                w = wide[u][:, :]
                                wait(e, s, f"load{u}", 16)
                                ch.add(e.tensor_scalar(cut[u][0][:, :], w, float(MOST), None, ALU.min)); ch.sync()
                                for p in range(1, PLANES):
                                    ch.add(e.tensor_tensor(w, w, cut[u][p - 1][:, :], ALU.subtract)); ch.sync()
                                    ch.add(e.tensor_copy(cut[u][p][:, :], w)); ch.sync()
                                e.sem_inc(s[f"cut{u}"])
        return flag


class Net:

    def __init__(self, nc, ctx):
        self.nc, self.ctx = nc, ctx
        sb = self.sb
        self.hT = sb("hT", [P, NP])
        self.xN = sb("xN", [P, NP])
        self.ident = sb("ident", [P, P])
        self.zero = sb("zero", [P, CW], BF16)
        self.eps = sb("eps", [P, 1])
        self.part = [sb(f"part{u}", [P, nb * P]) for u, (_, nb) in enumerate(PARTS)]
        self.ps = ctx.enter_context(nc.psum_tensor("ps", [P, 8, 512], F32))

    def use_counts(self, count, more, many):
        sb = self.sb
        self.count, self.more, self.many = count.rearrange("(s t) o -> s (t o)", t=PITCH), more, many
        self.aggT = sb("aggT", [P, NP])
        self.hN = sb("hN", [P, NP + HALF])
        self.ring = sb("ring", [P, SLOTS, HALF], F16)

    def sb(self, name, shape, dt=F32):
        return self.ctx.enter_context(self.nc.sbuf_tensor(name, shape, dt))

    def room(self, n):
        return self.hN[:, n * CW:(n + 1) * CW]


    def setup(self, x, matrices, vectors, directs):
        nc, P_ = self.nc, P
        full = (N // P) * P
        nm = len(matrices)
        with ExitStack() as tmp:
            raw = scratch(nc, tmp, "raw", [P, nm, P])
            with stage(nc, "id0", "cst", "x0", "x1", "w", "v", "tr", "cp") as (block, s):
                @block.gpsimd
                def _(e):
                    e.memset(self.ident[:, :], 0.0).then_inc(s["id0"], 1)
                    wait(e, s, "id0", 1)
                    e.affine_select(out=self.ident[:, :], in_=self.ident[:, :], compare_op=ALU.not_equal, fill=1.0,
                                    base=0, pattern=[[-1, P]], channel_multiplier=1).then_inc(s["cst"], 1)
                    e.memset(self.zero[:, :], 0.0).then_inc(s["cst"], 1)
                    e.memset(self.eps[:, :], LN_EPS).then_inc(s["cst"], 1)
                    wait(e, s, "cst", 3)

                @block.scalar
                def _(e):
                    e.dma_start(self.xN[:, 0:full].rearrange("p (k f) -> p k f", f=D),
                                x[0:full, :].rearrange("(k p) f -> p k f", p=P)).then_inc(s["x1"], 16)
                    for i, m in enumerate(matrices):
                        e.dma_start(raw[:, i, :], m).then_inc(s["w"], 16)
                    wait(e, s, "x0", 1)
                    e.dma_start(self.xN[0:N - full, full:NP], x[full:N, :]).then_inc(s["x1"], 16)
                    with nc.allow_non_contiguous_dma(reason="vectors of 128 words, one to a partition"):
                        for tile, v in vectors:
                            e.dma_start(tile, v).then_inc(s["v"], 16)
                    for tile, v in directs:
                        e.dma_start(tile, v).then_inc(s["v"], 16)
                    wait(e, s, "x1", 32)
                    wait(e, s, "v", 16 * (len(vectors) + len(directs)))

                @block.vector
                def _(e):
                    e.memset(self.xN[:, full:NP], 0.0).then_inc(s["x0"], 1)
                    for i in range(nm):
                        wait(e, s, "tr", i + 1)
                        e.tensor_copy(self.wT[:, i, :], self.ps[:, i % 8, 0:P]).then_inc(s["cp"], 1)
                    wait(e, s, "cp", nm)

                @block.tensor
                def _(e):
                    wait(e, s, "cst", 3)
                    wait(e, s, "w", 16 * nm)
                    for i in range(nm):
                        if i >= 8:
                            wait(e, s, "cp", i - 7)
                        e.transpose(self.ps[:, i % 8, 0:P], raw[:, i, :], self.ident[:, :]).then_inc(s["tr"], 1)

    @staticmethod
    def rsqrt(ch, y, var, root, t):
        e = ch.engine
        ch.add(e.reciprocal(y, root)); ch.sync()
        ch.add(e.tensor_tensor(t, y, y, ALU.mult)); ch.sync()
        ch.add(e.scalar_tensor_tensor(t, var, LN_EPS, t, ALU.add, ALU.mult)); ch.sync()
        ch.add(e.tensor_scalar(t, t, -0.5, 1.5, ALU.mult, ALU.add)); ch.sync()
        ch.add(e.tensor_tensor(y, y, t, ALU.mult)); ch.sync()


    def norm(self, add):
        nc, ps = self.nc, self.ps
        names = ["passed", "dve", "stats", "root"] + pairs("cut", "normed")
        credited = pairs(*["turned", "added"] * add, "turned_h", "stored")
        with ExitStack() as tmp, stage(nc, *names, credited=credited) as (block, s):
            rest = [scratch(nc, tmp, f"rest{u}", [P, nb * P]) for u, (_, nb) in enumerate(PARTS)]
            stats = [scratch(nc, tmp, f"stats{u}", [P, nb, 6]) for u, (_, nb) in enumerate(PARTS)]
            mv_slab = scratch(nc, tmp, "mv_slab", [P, SLAB_BLOCKS, 2])
            mv = scratch(nc, tmp, "mv", [P, 2 * NB])
            mean, var = (mv[:, :].rearrange("p (k t) -> p k t", t=2)[:, :, n] for n in (0, 1))
            root = scratch(nc, tmp, "root", [P, NB])
            inv = scratch(nc, tmp, "inv", [P, NB])
            tmp1 = scratch(nc, tmp, "tmp1", [P, NB])

            def cols(i, u):
                b0, nb = PARTS[u]
                return bass.ds(i * SLAB + b0 * P, nb * P)

            @block.tensor
            def _(e):
                if add:
                    with e.Fori(0, NSLAB) as i:
                        for u, (_, nb) in enumerate(PARTS):
                            wait(e, s, f"cut{u}", i + 1)
                            wait(e, s, f"added{u}", i)
                            for b in range(nb):
                                ins = e.transpose(ps[:, u, b * P:(b + 1) * P], self.part[u][:, b * P:(b + 1) * P],
                                                  self.ident[:, :])
                            ins.then_inc(s[f"turned{u}"], 1)
                with e.Fori(0, NSLAB) as i:
                    for u, (_, nb) in enumerate(PARTS):
                        wait(e, s, f"normed{u}", i + 1)
                        wait(e, s, f"stored{u}", i)
                        for b in range(nb):
                            ins = e.transpose(ps[:, 2 + u, b * P:(b + 1) * P], rest[u][:, b * P:(b + 1) * P],
                                              self.ident[:, :])
                        ins.then_inc(s[f"turned_h{u}"], 1)

            @block.vector
            def _(e):
                ch = Chain(e, s["dve"])
                with e.Fori(0, NSLAB) as i:
                    if add:
                        for u, (b0, nb) in enumerate(PARTS):
                            wait(e, s, f"turned{u}", i + 1)
                            ch.add(e.tensor_tensor(self.xN[:, cols(i, u)], ps[:, u, 0:nb * P], self.xN[:, cols(i, u)],
                                                   ALU.add))
                        ch.sync()
                        for u in (0, 1):
                            e.sem_inc(s[f"added{u}"])
                    for u, (b0, nb) in enumerate(PARTS):
                        for b in range(nb):
                            ch.add(e.bn_stats(stats[u][:, b, :], self.xN[:, bass.ds(i * SLAB + (b0 + b) * P, P)]))
                    ch.sync()
                    for u, (b0, nb) in enumerate(PARTS):
                        for b in range(nb):
                            ch.add(e.bn_aggr(mv_slab[:, b0 + b, :], stats[u][:, b, :]))
                    ch.sync()
                    ch.add(e.tensor_copy(mv[:, bass.ds(i * (2 * SLAB_BLOCKS), 2 * SLAB_BLOCKS)],
                                         mv_slab[:, :, :].rearrange("p b t -> p (b t)")))
                    ch.restart()
                e.sem_inc(s["stats"])
                e.wait_ge(s["root"], 1)
                self.rsqrt(ch, inv[:, :], var, root[:, :], tmp1[:, :])
                ch.restart()
                with e.Fori(0, NSLAB) as i:
                    for u, (b0, nb) in enumerate(PARTS):
                        wait(e, s, f"turned_h{u}", i)
                        for b in range(nb):
                            k = i * SLAB_BLOCKS + b0 + b
                            ch.add(e.tensor_scalar(rest[u][:, b * P:(b + 1) * P],
                                                   self.xN[:, bass.ds(i * SLAB + (b0 + b) * P, P)],
                                                   mv[:, bass.ds(k * 2, 1)], inv[:, bass.ds(k, 1)],
                                                   ALU.subtract, ALU.mult))
                        ch.sync()
                        e.sem_inc(s[f"normed{u}"])
                    ch.restart()

            @block.scalar
            def _(e):
                if add:
                    with e.Fori(0, NSLAB) as i:
                        for u in (0, 1):
                            wait(e, s, f"turned{u}", i)
                            e.copy(self.part[u][:, :], self.hT[:, cols(i, u)]).then_inc(s[f"cut{u}"], 1)
                e.wait_ge(s["stats"], 1)
                e.activation(root[:, :], var, ACT.Sqrt, bias=self.eps[:, 0:1]).then_inc(s["root"], 1)
                with e.Fori(0, NSLAB) as i:
                    for u, (b0, nb) in enumerate(PARTS):
                        wait(e, s, f"turned_h{u}", i + 1)
                        e.activation(self.hT[:, cols(i, u)], ps[:, 2 + u, 0:nb * P], ACT.Relu)\
                            .then_inc(s[f"stored{u}"], 1)


    def messages(self, msg, w, bias, column_bias, column_out):
        nc, ps = self.nc, self.ps
        with stage(nc, "passed", "dve", *pairs("cut"), credited=pairs("made", "taken")) as (block, s):
            def cols(i, u):
                b0, nb = PARTS[u]
                return bass.ds(i * SLAB + b0 * P, nb * P)

            @block.scalar
            def _(e):
                with e.Fori(0, NSLAB) as i:
                    for u in (0, 1):
                        wait(e, s, f"made{u}", i)
                        e.copy(self.part[u][:, :], self.hT[:, cols(i, u)]).then_inc(s[f"cut{u}"], 1)

            @block.tensor
            def _(e):
                with e.Fori(0, NSLAB) as i:
                    for u, (_, nb) in enumerate(PARTS):
                        wait(e, s, f"cut{u}", i + 1)
                        wait(e, s, f"taken{u}", i)
                        for b in range(nb):
                            o = b % 2 * (D + 1)
                            ins = e.matmul(ps[:, 2 * u + b // 2, o:o + D + 1],
                                           self.part[u][:, b * P:(b + 1) * P], w, start=True, stop=True)
                        ins.then_inc(s[f"made{u}"], 1)

            @block.vector
            def _(e):
                ch = Chain(e, s["dve"])
                with e.Fori(0, NSLAB) as i:
                    for u, (b0, nb) in enumerate(PARTS):
                        wait(e, s, f"made{u}", i + 1)
                        for g in (0, 1):
                            n, k = min(2, nb - 2 * g), i * SLAB_BLOCKS + b0 + 2 * g
                            made = ps[:, 2 * u + g, 0:n * (D + 1)].rearrange("p (b f) -> p b f", f=D + 1)
                            out = msg[:, bass.ds(k * P, n * P)].rearrange("p (b f) -> p b f", f=P)
                            b3 = bias.rearrange("p (a f) -> p a f", a=1).to_broadcast([P, n, P])
                            ch.add(e.tensor_tensor(out, made[:, :, 0:D], b3, ALU.add))
                            ch.add(e.tensor_scalar(column_out[:, bass.ds(k, n)].rearrange("p (b a) -> p b a", a=1),
                                                   made[:, :, D:D + 1], column_bias, None, ALU.add))
                        ch.sync()
                        e.sem_inc(s[f"taken{u}"])
                    ch.restart()


    def stream_counts(self, e, s, plane=0):
        if isinstance(plane, int):
            table, row = self.count, 0
        else:
            table, row = self.more, (plane - 1) * NP
        with e.Fori(0, 2) as half:
            with e.Fori(0, NB // SLOTS) as kk:
                for j in range(SLOTS):
                    wait(e, s, f"free{j}", half * (NB // SLOTS) + kk)
                    e.dma_start(self.ring[:, j, :],
                                table[bass.ds(row + kk * (SLOTS * P) + j * P, P), bass.ds(half * HALF, HALF)])\
                        .then_inc(s[f"slot{j}"], 16)
        for j in range(SLOTS):
            wait(e, s, f"free{j}", 2 * (NB // SLOTS))

    def aggregate(self, w=None, add_self=False, load=(), prepare_act=None, prepare_dve=None):
        self.sum_over(0, w, add_self, load, prepare_act, prepare_dve)
        self.other_planes(self.sum_over)

    def sum_over(self, plane, w=None, add_self=False, load=(), prepare_act=None, prepare_dve=None):
        nc, ps = self.nc, self.ps
        turns = NB // SLOTS
        first = isinstance(plane, int)
        assert SLOTS == SLAB_BLOCKS and HC == 7
        SPARE = 7
        names = ["passed", "small", "root", "dve"]\
            + [f"{n}{j}" for n in ("slot", "high", "hi", "lo") for j in range(SLOTS)]\
            + [f"wide{g}" for g in range(len(WIDENERS))] + pairs("cut")
        credited = [f"used{g}" for g in range(len(WIDENERS))] + [f"out{c}" for c in range(HC)] + pairs("made", "kept")
        with ExitStack() as tmp, stage(nc, *names, credited=credited) as (block, s):
            wide = scratch(nc, tmp, "wide", [P, 2, HALF], F32R)
            high = scratch(nc, tmp, "high", [P, SLOTS, P], I32)
            hi = scratch(nc, tmp, "hi", [P, SLOTS, P], F32R)
            lo = scratch(nc, tmp, "lo", [P, SLOTS, P], F32R)

            def cols(i, u):
                b0, nb = PARTS[u]
                return bass.ds(i * SLAB + b0 * P, nb * P)

            def node_block(kk, j):
                return self.hN[:, bass.ds(kk * SLAB + j * P, P)]

            def run(e, body, begin=lambda half: None, end=lambda half: None):
                begin(0)
                loops = turns - 1 if first else turns
                with e.Fori(0, loops) as kk:
                    body(kk, kk, first)
                if first:
                    body(turns - 1, turns - 1, False)
                end(0)
                begin(1)
                with e.Fori(0, turns) as kk:
                    body(kk + turns, kk, False)
                end(1)

            def widen(e, name, t, j):
                number = t * SLOTS + j
                wait(e, s, f"slot{j}", t * 16 + 16)
                copy = e.copy if name == "scalar" else e.tensor_copy
                for g, (owner, c0, n) in enumerate(WIDENERS):
                    if owner == name:
                        wait(e, s, f"used{g}", number if j == 0 else number - 1)
                        copy(wide[:, j % 2, c0 * CW:(c0 + n) * CW], self.ring[:, j, c0 * CW:(c0 + n) * CW])\
                            .then_inc(s[f"wide{g}"], 1)

            @block.sync
            def _(e):
                table, row = (self.count, 0) if first else (self.more, (plane - 1) * NP)
                with nc.allow_non_contiguous_dma(reason="vectors of 128 words, one to a partition"):
                    for tile, source in load:
                        e.dma_start(tile, source).then_inc(s["small"], 16)

                def rows_in(t, kk, j, half):
                    e.dma_start(self.ring[:, j, :],
                                table[bass.ds(row + kk * (SLOTS * P) + j * P, P), bass.ds(half * HALF, HALF)])\
                        .then_inc(s[f"slot{j}"], 16)

                for j in range(SLOTS):
                    rows_in(0, 0, j, 0)
                for half in (0, 1):
                    with e.Fori(1 - half, turns) as kk:
                        t = kk + half * turns
                        for j in range(SLOTS):
                            for g in range(len(WIDENERS)):
                                wait(e, s, f"wide{g}", t * SLOTS + (j + 1 - SLOTS))
                            rows_in(t, kk, j, half)
                for g in range(len(WIDENERS)):
                    wait(e, s, f"wide{g}", 2 * NB)
                if load:
                    e.wait_ge(s["small"], 16 * len(load))

            @block.gpsimd
            def _(e):
                def cut(i, u):
                    wait(e, s, f"made{u}", i)
                    e.tensor_copy(self.part[u][:, :], self.hT[:, cols(i, u)]).then_inc(s[f"cut{u}"], 1)

                def turn(t, kk, next_slab):
                    for j in range(SLOTS):
                        if next_slab and j in (0, 3):
                            cut(kk + 1, int(j == 3))
                        wait(e, s, f"high{j}", t + 1)
                        e.tensor_tensor(lo[:, j, :], node_block(kk, j), high[:, j, :].bitcast(F32), ALU.subtract)\
                            .then_inc(s[f"lo{j}"], 1)

                run(e, turn)

            @block.tensor
            def _(e):
                def product(i, u):
                    wait(e, s, f"cut{u}", i + 1)
                    if u == 0:
                        wait(e, s, "kept1", i)
                    else:
                        wait(e, s, "kept0", i + 1)
                    for b in range(PARTS[u][1]):
                        o = ps[:, SPARE, b * P:(b + 1) * P]
                        piece = self.part[u][:, b * P:(b + 1) * P]
                        if w is None:
                            ins = e.transpose(o, piece, self.ident[:, :])
                        else:
                            ins = e.matmul(o, piece, w, start=True, stop=True)
                    ins.then_inc(s[f"made{u}"], 1)

                def turn(t, kk, next_slab):
                    for j in range(SLOTS):
                        wait(e, s, f"hi{j}", t + 1)
                        wait(e, s, f"lo{j}", t + 1)
                        for g, (_, c0, n) in enumerate(WIDENERS):
                            wait(e, s, f"wide{g}", t * SLOTS + j + 1)
                            for part in (hi, lo):
                                for c in range(c0, c0 + n):
                                    ins = e.matmul(ps[:, c, 0:CW], part[:, j, :], wide[:, j % 2, c * CW:(c + 1) * CW],
                                                   start=False, stop=True, skip_group_check=True)
                            ins.then_inc(s[f"used{g}"], 1)
                        if next_slab and j in (0, 3):
                            product(kk + 1, int(j == 3))

                def clear(half):
                    for c in range(HC):
                        wait(e, s, f"out{c}", half)
                        e.matmul(ps[:, c, 0:CW], self.zero[:, 0:P], self.zero[:, :], start=True, stop=True)

                if w is not None and load:
                    e.wait_ge(s["small"], 16 * len(load))
                if first:
                    product(0, 0)
                    product(0, 1)
                run(e, turn, begin=clear)

            def take(e, half, chunks):
                for g, (_, c0, n) in enumerate(WIDENERS):
                    wait(e, s, f"used{g}", half * NB + NB)
                    for c in range(c0, c0 + n):
                        if c in chunks:
                            o = slice(half * HALF + c * CW, half * HALF + (c + 1) * CW)
                            agg = self.aggT[:, o]
                            if add_self or not first:
                                ins = e.tensor_tensor(agg, ps[:, c, 0:CW], self.hT[:, o] if first else agg, ALU.add)
                            else:
                                ins = (e.copy if e is nc.scalar else e.tensor_copy)(agg, ps[:, c, 0:CW])
                            ins.then_inc(s[f"out{c}"], 1)

            alone = add_self or not first
            shares = ([], range(HC)) if alone else (range(1, HC, 2), range(0, HC, 2))

            @block.scalar
            def _(e):
                def keep(i, u):
                    wait(e, s, f"made{u}", i + 1)
                    e.copy(self.hN[:, cols(i, u)], ps[:, SPARE, 0:PARTS[u][1] * P]).then_inc(s[f"kept{u}"], 1)

                def turn(t, kk, next_slab):
                    for j in range(SLOTS):
                        wait(e, s, f"high{j}", t + 1)
                        e.copy(hi[:, j, :], high[:, j, :].bitcast(F32)).then_inc(s[f"hi{j}"], 1)
                        widen(e, "scalar", t, j)
                        if next_slab and j in (2, 5):
                            keep(kk + 1, int(j == 5))

                if first:
                    for u in (0, 1):
                        e.copy(self.part[u][:, :], self.hT[:, cols(0, u)]).then_inc(s[f"cut{u}"], 1)
                    keep(0, 0)
                    keep(0, 1)
                run(e, turn, end=lambda half: take(e, half, shares[0]))
                if prepare_act is not None:
                    e.wait_ge(s["small"], 16 * len(load))
                    prepare_act(e, s["root"])

            @block.vector
            def _(e):
                def turn(t, kk, next_slab):
                    for j in range(SLOTS):
                        if first and isinstance(t, int) or next_slab:
                            for u, (b0, _) in enumerate(PARTS):
                                if j == b0:
                                    wait(e, s, f"kept{u}", kk + 1)
                        e.tensor_scalar(high[:, j, :], node_block(kk, j).bitcast(I32), HIGH_BITS, None,
                                        ALU.bitwise_and).then_inc(s[f"high{j}"], 1)
                        widen(e, "vector", t, j)

                run(e, turn, end=lambda half: take(e, half, shares[1]))
                if prepare_dve is not None:
                    e.wait_ge(s["root"], 1)
                    prepare_dve(Chain(e, s["dve"]))

    def other_planes(self, body):
        nc = self.nc
        with nc.If(self.many > 0):
            with nc.Fori(1, PLANES) as plane:
                body(plane)


    def dense(self, source, layers, target, first_relu=False):
        nc, ps = self.nc, self.ps
        L = len(layers)
        credited = pairs(*[f"mm{n}_" for n in range(L)], *[f"act{n}_" for n in range(1, L + 1)])
        with stage(nc, "passed", "act", *pairs("act0_"), credited=credited) as (block, s):
            mid = [[self.room(2 * n + u) for u in (0, 1)] for n in range(L)]

            def cols(i, u):
                return bass.ds(i * (2 * CW) + u * CW, CW)

            @block.tensor
            def _(e):
                with e.Fori(0, NCH // 2) as i:
                    for n, (w, _, _, _) in enumerate(layers):
                        for u in (0, 1):
                            if n > 0 or first_relu:
                                wait(e, s, f"act{n}_{u}", i + 1)
                            wait(e, s, f"act{n + 1}_{u}", i)
                            rhs = mid[n][u][:, :] if n > 0 or first_relu else source[:, cols(i, u)]
                            e.matmul(ps[:, 2 * n + u, 0:CW], w, rhs, start=True, stop=True).then_inc(s[f"mm{n}_{u}"], 1)

            @block.scalar
            def _(e):
                ch = Chain(e, s["act"])
                with e.Fori(0, NCH // 2) as i:
                    if first_relu:
                        for u in (0, 1):
                            wait(e, s, f"mm0_{u}", i)
                            ch.add(e.activation(mid[0][u][:, :], source[:, cols(i, u)], ACT.Relu))
                            ch.sync()
                            e.sem_inc(s[f"act0_{u}"])
                    for n, (_, func, scale, bias) in enumerate(layers):
                        for u in (0, 1):
                            wait(e, s, f"mm{n}_{u}", i + 1)
                            if n + 1 < L:
                                wait(e, s, f"mm{n + 1}_{u}", i)
                            out = mid[n + 1][u][:, :] if n + 1 < L else target[:, cols(i, u)]
                            ch.add(e.activation(out, ps[:, 2 * n + u, 0:CW], func, scale=scale, bias=bias))
                            ch.sync()
                            e.sem_inc(s[f"act{n + 1}_{u}"])
                    ch.restart()

    def gru(self, w_in, w_state, b_in, b_state, b_sum):
        nc, ps = self.nc, self.ps
        with stage(nc, "passed", "dve", "act", *pairs("mm", "rz", "new"), credited=pairs("pre", "next")) as (block, s):
            r, z, pre, new = [[self.room(2 * n + u) for u in (0, 1)] for n in range(4)]

            def cols(i, u):
                return bass.ds(i * (2 * CW) + u * CW, CW)

            @block.tensor
            def _(e):
                with e.Fori(0, NCH // 2) as i:
                    for u in (0, 1):
                        wait(e, s, f"pre{u}", i)
                        c, b = cols(i, u), 4 * u
                        for g in (0, 1):
                            e.matmul(ps[:, b + g, 0:CW], w_in[g], self.aggT[:, c], start=True, stop=False)
                            e.matmul(ps[:, b + g, 0:CW], w_state[g], self.hT[:, c], start=False, stop=True)
                        e.matmul(ps[:, b + 3, 0:CW], w_state[2], self.hT[:, c], start=True, stop=True)
                        e.matmul(ps[:, b + 2, 0:CW], w_in[2], self.aggT[:, c], start=True, stop=True)\
                            .then_inc(s[f"mm{u}"], 1)

            @block.scalar
            def _(e):
                ch = Chain(e, s["act"])
                with e.Fori(0, NCH // 2) as i:
                    for u in (0, 1):
                        wait(e, s, f"mm{u}", i + 1)
                        wait(e, s, f"next{u}", i)
                        ch.add(e.activation(r[u][:, :], ps[:, 4 * u, 0:CW], ACT.Sigmoid, bias=b_sum[0]))
                        ch.add(e.activation(z[u][:, :], ps[:, 4 * u + 1, 0:CW], ACT.Sigmoid, bias=b_sum[1]))
                        ch.sync()
                        e.sem_inc(s[f"rz{u}"])
                    for u in (0, 1):
                        wait(e, s, f"pre{u}", i + 1)
                        ch.add(e.activation(new[u][:, :], pre[u][:, :], ACT.Tanh, bias=b_in[2]))
                        ch.sync()
                        e.sem_inc(s[f"new{u}"])
                    ch.restart()

            @block.vector
            def _(e):
                ch = Chain(e, s["dve"])
                with e.Fori(0, NCH // 2) as i:
                    for u in (0, 1):
                        wait(e, s, f"rz{u}", i + 1)
                        ch.add(e.scalar_tensor_tensor(pre[u][:, :], ps[:, 4 * u + 3, 0:CW], b_state[2], r[u][:, :],
                                                      ALU.add, ALU.mult))
                        ch.sync()
                        ch.add(e.tensor_tensor(pre[u][:, :], ps[:, 4 * u + 2, 0:CW], pre[u][:, :], ALU.add))
                        ch.sync()
                        e.sem_inc(s[f"pre{u}"])
                    for u in (0, 1):
                        c = cols(i, u)
                        wait(e, s, f"new{u}", i + 1)
                        ch.add(e.tensor_tensor(self.hT[:, c], self.hT[:, c], new[u][:, :], ALU.subtract))
                        ch.sync()
                        ch.add(e.tensor_tensor(self.hT[:, c], self.hT[:, c], z[u][:, :], ALU.mult))
                        ch.sync()
                        ch.add(e.tensor_tensor(self.hT[:, c], self.hT[:, c], new[u][:, :], ALU.add))
                        ch.sync()
                        e.sem_inc(s[f"next{u}"])
                    ch.restart()


    def target_scores(self, w_rep, scores):
        nc, ps = self.nc, self.ps
        with stage(nc, "passed", *pairs("mm"), credited=pairs("out")) as (block, s):
            def cols(i, u):
                return bass.ds(i * (2 * CW) + u * CW, CW)

            @block.tensor
            def _(e):
                with e.Fori(0, NCH // 2) as i:
                    for u in (0, 1):
                        wait(e, s, f"out{u}", i)
                        e.matmul(ps[:, u, 0:CW], w_rep, self.hT[:, cols(i, u)], start=True, stop=True)\
                            .then_inc(s[f"mm{u}"], 1)

            @block.vector
            def _(e):
                with e.Fori(0, NCH // 2) as i:
                    for u in (0, 1):
                        wait(e, s, f"mm{u}", i + 1)
                        e.tensor_copy(scores[:, cols(i, u)], ps[:, u, 0:CW]).then_inc(s[f"out{u}"], 1)

    def attend(self, msg, scores, source_scores, gate_room, plane=0):
        nc, ps = self.nc, self.ps
        turns = NB // SLOTS
        names = ["passed", f"used_cut{SLOTS - 1}"] + [f"{n}{j}" for n in ("cut", "slot") for j in range(SLOTS)]\
            + [f"{n}{c}" for n in ("gate", "weighed") for c in range(HC)]
        credited = [f"free{j}" for j in range(SLOTS)] + [f"used_cut{j}" for j in range(SLOTS - 1)]\
            + [f"{n}{c}" for n in ("out", "used") for c in range(HC)]
        with ExitStack() as tmp, stage(nc, *names, credited=credited) as (block, s):
            gate = gate_room.rearrange("p (c t) -> p c t", t=CW)
            piece = scratch(nc, tmp, "piece", [P, SLOTS, P])

            @block.sync
            def _(e):
                self.stream_counts(e, s, plane)

            @block.gpsimd
            def _(e):
                with e.Fori(0, 2) as half:
                    with e.Fori(0, turns) as kk:
                        for j in range(SLOTS):
                            wait(e, s, f"used_cut{j}", half * turns + kk + (j == SLOTS - 1))
                            e.tensor_copy(piece[:, j, :], msg[:, bass.ds(kk * (SLOTS * P) + j * P, P)])\
                                .then_inc(s[f"cut{j}"], 1)

            @block.scalar
            def _(e):
                with e.Fori(0, 2) as half:
                    with e.Fori(0, turns) as kk:
                        for j in range(SLOTS):
                            n = half * NB + kk * SLOTS + j
                            for c in range(HC):
                                wait(e, s, f"used{c}", n)
                                e.activation(gate[:, c, :], scores[:, bass.ds(half * HALF + c * CW, CW)], ACT.Sigmoid,
                                             bias=source_scores[:, bass.ds(kk * SLOTS + j, 1)])\
                                    .then_inc(s[f"gate{c}"], 1)

            @block.vector
            def _(e):
                with e.Fori(0, 2) as half:
                    with e.Fori(0, turns) as kk:
                        for j in range(SLOTS):
                            n = half * NB + kk * SLOTS + j
                            wait(e, s, f"slot{j}", half * (16 * turns) + kk * 16 + 16)
                            for c in range(HC):
                                wait(e, s, f"gate{c}", n + 1)
                                ins = e.tensor_tensor(gate[:, c, :], gate[:, c, :], self.ring[:, j, c * CW:(c + 1) * CW],
                                                      ALU.mult).then_inc(s[f"weighed{c}"], 1)
                            wait(e, s, f"weighed{HC - 1}", n + 1)
                            e.sem_inc(s[f"free{j}"])
                    wait(e, s, f"used{HC - 1}", half * NB + NB)
                    for c in range(HC):
                        agg = self.aggT[:, bass.ds(half * HALF + c * CW, CW)]
                        if isinstance(plane, int):
                            ins = e.tensor_copy(agg, ps[:, c, 0:CW])
                        else:
                            ins = e.tensor_tensor(agg, ps[:, c, 0:CW], agg, ALU.add)
                        ins.then_inc(s[f"out{c}"], 1)

            @block.tensor
            def _(e):
                with e.Fori(0, 2) as half:
                    for c in range(HC):
                        wait(e, s, f"out{c}", half)
                        e.matmul(ps[:, c, 0:CW], self.zero[:, 0:P], self.zero[:, :], start=True, stop=True)
                    with e.Fori(0, turns) as kk:
                        for j in range(SLOTS):
                            n = half * NB + kk * SLOTS + j
                            wait(e, s, f"cut{j}", half * turns + kk + 1)
                            for c in range(HC):
                                wait(e, s, f"weighed{c}", n + 1)
                                ins = e.matmul(ps[:, c, 0:CW], piece[:, j, :], gate[:, c, :], start=False, stop=True,
                                               skip_group_check=True)
                                ins.then_inc(s[f"used{c}"], 1)
                                if c == HC // 2:
                                    wait(e, s, f"used{HC - 1}", n)
                                    e.sem_inc(s[f"used_cut{(j - 1) % SLOTS}"])

    def batch_norm(self, gamma, beta):
        nc = self.nc
        W = 250
        assert N % (5 * W) == 0
        with ExitStack() as tmp, stage(nc, "passed", "dve", "stats", "root", "inv", "done") as (block, s):
            def sb(n, shape):
                return scratch(nc, tmp, n, shape)
            stats, mv = sb("bn_st", [P, (N // W) * 6]), sb("bn_mv", [P, 2])
            root, inv, t, scale, shift = (sb(f"bn_{n}", [P, 1]) for n in ("root", "inv", "t", "scale", "shift"))

            @block.vector
            def _(e):
                ch = Chain(e, s["dve"])
                with e.Fori(0, N // W // 5) as i:
                    for j in range(5):
                        e.bn_stats(stats[:, bass.ds(i * 30 + j * 6, 6)], self.hT[:, bass.ds(i * (5 * W) + j * W, W)])\
                            .then_inc(s["stats"], 1)
                wait(e, s, "stats", N // W)
                ch.add(e.bn_aggr(mv[:, :], stats[:, :])); ch.sync()
                e.sem_inc(s["stats"])
                wait(e, s, "root", 1)
                self.rsqrt(ch, inv[:, :], mv[:, 1:2], root[:, :], t[:, :])
                ch.add(e.tensor_tensor(scale[:, :], gamma, inv[:, :], ALU.mult)); ch.sync()
                ch.add(e.scalar_tensor_tensor(shift[:, :], mv[:, 0:1], -1.0, scale[:, :], ALU.mult, ALU.mult)); ch.sync()
                ch.add(e.tensor_tensor(shift[:, :], shift[:, :], beta, ALU.add)); ch.sync()
                e.sem_inc(s["inv"])

            @block.scalar
            def _(e):
                wait(e, s, "stats", N // W + 1)
                e.activation(root[:, :], mv[:, 1:2], ACT.Sqrt, bias=self.eps[:, 0:1]).then_inc(s["root"], 1)
                wait(e, s, "inv", 1)
                with e.Fori(0, NSLAB) as i:
                    e.activation(self.hT[:, bass.ds(i * SLAB, SLAB)], self.hT[:, bass.ds(i * SLAB, SLAB)], ACT.Identity,
                                 scale=scale[:, 0:1], bias=shift[:, 0:1]).then_inc(s["done"], 1)
                wait(e, s, "done", NSLAB)


    def finish(self, out):
        nc, ps = self.nc, self.ps
        full = (N // P) * P
        with stage(nc, "passed", "store", *pairs("cut"), credited=pairs("turned", "added")) as (block, s):
            def cols(i, u):
                b0, nb = PARTS[u]
                return bass.ds(i * SLAB + b0 * P, nb * P)

            @block.scalar
            def _(e):
                with e.Fori(0, NSLAB) as i:
                    for u in (0, 1):
                        wait(e, s, f"turned{u}", i)
                        e.copy(self.part[u][:, :], self.hT[:, cols(i, u)]).then_inc(s[f"cut{u}"], 1)

            @block.tensor
            def _(e):
                with e.Fori(0, NSLAB) as i:
                    for u, (_, nb) in enumerate(PARTS):
                        wait(e, s, f"cut{u}", i + 1)
                        wait(e, s, f"added{u}", i)
                        for b in range(nb):
                            ins = e.transpose(ps[:, u, b * P:(b + 1) * P], self.part[u][:, b * P:(b + 1) * P],
                                              self.ident[:, :])
                        ins.then_inc(s[f"turned{u}"], 1)

            @block.vector
            def _(e):
                with e.Fori(0, NSLAB) as i:
                    for u, (b0, nb) in enumerate(PARTS):
                        wait(e, s, f"turned{u}", i + 1)
                        e.tensor_tensor(self.xN[:, cols(i, u)], ps[:, u, 0:nb * P], self.xN[:, cols(i, u)], ALU.add)\
                            .then_inc(s[f"added{u}"], 1)

            @block.sync
            def _(e):
                with e.Fori(0, NSLAB - 1) as i:
                    for u in (0, 1):
                        wait(e, s, f"added{u}", i + 1)
                    e.dma_start(out[bass.ds(i * SLAB, SLAB), :].rearrange("(k p) f -> p k f", p=P),
                                self.xN[:, bass.ds(i * SLAB, SLAB)].rearrange("p (k f) -> p k f", f=D))\
                        .then_inc(s["store"], 16)
                last = (NSLAB - 1) * SLAB
                for u in (0, 1):
                    wait(e, s, f"added{u}", NSLAB)
                e.dma_start(out[last:full, :].rearrange("(k p) f -> p k f", p=P),
                            self.xN[:, last:full].rearrange("p (k f) -> p k f", f=D)).then_inc(s["store"], 16)
                e.dma_start(out[full:N, :], self.xN[0:N - full, full:NP]).then_inc(s["store"], 16)
                wait(e, s, "store", 16 * (NSLAB + 1))


def program(nc, a, out):
    count = nc.dram_tensor("count", [PLANE_ROWS * PITCH, 1], F16, kind="Internal").ap()
    more = nc.dram_tensor("more", [(PLANES - 1) * NP, PITCH], F16, kind="Internal").ap()
    with ExitStack() as ctx:
        net = Net(nc, ctx)
        sb = net.sb
        many = sb("many", [P, 1], I32)

        def gates(m):
            return [m[g * D:(g + 1) * D, :] for g in range(3)]

        names, matrices = {}, []
        for key, blocks in (("1ih", gates(a["L1_gnn_W_ih"])), ("1hh", gates(a["L1_gnn_W_hh"])),
                            ("2e1", [a["L2_gnn_enc_w1"]]), ("2e2", [a["L2_gnn_enc_w2"]]),
                            ("2ih", gates(a["L2_gnn_gru_wih"])), ("2hh", gates(a["L2_gnn_gru_whh"])),
                            ("2d1", [a["L2_gnn_dec_w1"]]), ("2d2", [a["L2_gnn_dec_w2"]]), ("3", [a["L3_gnn_W"]])):
            names[key] = range(len(matrices), len(matrices) + len(blocks))
            matrices += blocks

        def column(v):
            return v.rearrange("(p o) -> p o", o=1)

        def three(v):
            return v.rearrange("(g p) -> p g", p=P)

        b1i, b1h, b1s = sb("b1i", [P, 3]), sb("b1h", [P, 3]), sb("b1s", [P, 3])
        b2i, b2h, b2s = sb("b2i", [P, 3]), sb("b2h", [P, 3]), sb("b2s", [P, 3])
        gam, bet, e1, e2, d1, d2, b3 = (sb(n, [P, 1]) for n in ("gam", "bet", "e1", "e2", "d1", "d2", "b3"))
        w_att = sb("w_att", [P, 2])
        b_att = sb("b_att", [P, 1])
        b_msg = sb("b_msg", [P, D])
        w_msg = sb("w_msg", [P, D + 1])
        att_rep = sb("att_rep", [P, P])
        vectors = [(b1i[:, :], three(a["L1_gnn_b_ih"])), (b1h[:, :], three(a["L1_gnn_b_hh"])),
                   (b2i[:, :], three(a["L2_gnn_gru_bih"])), (b2h[:, :], three(a["L2_gnn_gru_bhh"])),
                   (gam[:, :], column(a["L1_gnn_gamma"])), (bet[:, :], column(a["L1_gnn_beta"])),
                   (e1[:, :], column(a["L2_gnn_enc_b1"])), (e2[:, :], column(a["L2_gnn_enc_b2"])),
                   (d1[:, :], column(a["L2_gnn_dec_b1"])), (d2[:, :], column(a["L2_gnn_dec_b2"])),
                   (b3[:, :], column(a["L3_gnn_b"])),
                   (w_msg[:, D:D + 1], a["L1_gnn_W_att"][0:D, :]),
                   (w_att[:, :], a["L1_gnn_W_att"].rearrange("(g p) o -> p (g o)", p=P)),
                   (b_att[:, :], a["L1_gnn_b_att"].rearrange("(a o) -> a o", a=1).to_broadcast([P, 1]))]
        directs = [(b_msg[:, :], a["L1_gnn_b_msg"].rearrange("(a f) -> a f", a=1).to_broadcast([P, D])),
                   (w_msg[:, 0:D], a["L1_gnn_W_msg"])]

        def wt(key):
            return [net.wT[:, i, :] for i in names[key]]

        net.wT = sb("wT", [P, len(matrices), P])

        net.setup(a["x"], matrices, vectors, directs)

        def before_counts():
            with stage(nc, "one") as (block, s):
                @block.vector
                def _(e):
                    e.tensor_tensor(b1s[:, :], b1i[:, :], b1h[:, :], ALU.add).then_inc(s["one"], 1)
                    e.tensor_tensor(b2s[:, :], b2i[:, :], b2h[:, :], ALU.add).then_inc(s["one"], 1)
                    e.tensor_copy(att_rep[:, :], w_att[:, 1:2].to_broadcast([P, P])).then_inc(s["one"], 1)
                    wait(e, s, "one", 3)
            net.norm(add=False)

        net.use_counts(count, more, build_counts(nc, a["src"], a["dst"], count, more, many[:, :], net.ps,
                                                 before_counts))

        w12 = sb("w12", [P, 2, D])
        vec = sb("vec", [P, 5, 2])
        bn = sb("bn", [P, 4, 2])
        layers0 = 3
        with nc.Fori(0, layers0) as layer:
            load = [(w12[:, n, :], m.rearrange("l i o -> (l i) o")[bass.ds(layer * D, D), :])
                    for n, m in enumerate((a["L0_gnn_W1"], a["L0_gnn_W2"]))]
            load += [(vec[:, 0, n:n + 1], v.rearrange("l (f o) -> (l f) o", o=1)[bass.ds(layer * D, D), :])
                     for n, v in enumerate((a["L0_gnn_b1"], a["L0_gnn_b2"]))]
            load += [(vec[:, 1 + q, n:n + 1],
                      v.rearrange("l n (f o) -> (l n f) o", o=1)[bass.ds(layer * (2 * D) + n * D, D), :])
                     for q, v in enumerate((a["L0_gnn_g"], a["L0_gnn_be"], a["L0_gnn_rm"], a["L0_gnn_rv"]))
                     for n in (0, 1)]

            def norm_roots(e, done):
                e.activation(bn[:, 0, :], vec[:, 4, :], ACT.Sqrt, bias=net.eps[:, 0:1]).then_inc(done, 1)

            def norm_factors(ch):
                e = ch.engine
                net.rsqrt(ch, bn[:, 1, :], vec[:, 4, :], bn[:, 0, :], bn[:, 2, :])
                ch.add(e.tensor_tensor(bn[:, 1, :], bn[:, 1, :], vec[:, 1, :], ALU.mult)); ch.sync()
                ch.add(e.tensor_tensor(bn[:, 3, :], vec[:, 0, :], vec[:, 3, :], ALU.subtract)); ch.sync()
                ch.add(e.tensor_tensor(bn[:, 3, :], bn[:, 3, :], bn[:, 1, :], ALU.mult)); ch.sync()
                ch.add(e.tensor_tensor(bn[:, 3, :], bn[:, 3, :], vec[:, 2, :], ALU.add)); ch.sync()

            net.aggregate(add_self=True, load=load, prepare_act=norm_roots, prepare_dve=norm_factors)
            net.dense(net.aggT, [(w12[:, n, :], ACT.Relu, bn[:, 1, n:n + 1], bn[:, 3, n:n + 1]) for n in (0, 1)], net.hT)

        net.norm(add=True)
        source_scores = sb("source_scores", [P, NB])
        scores = net.hN[:, 0:NP]
        gate_room = net.hN[:, NP:NP + HALF]
        with nc.sbuf_tensor("msg", [P, NP], F32) as msg:
            net.messages(msg, w_msg[:, :], b_msg[:, :], b_att[:, 0:1], source_scores)
            net.target_scores(att_rep[:, :], scores)
            net.attend(msg, scores, source_scores, gate_room)
            net.other_planes(lambda plane: net.attend(msg, scores, source_scores, gate_room, plane))
        net.gru(wt("1ih"), wt("1hh"), [b1i[:, g:g + 1] for g in range(3)], [b1h[:, g:g + 1] for g in range(3)],
                [b1s[:, g:g + 1] for g in range(3)])
        net.batch_norm(gam[:, :], bet[:, :])

        net.norm(add=True)
        net.dense(net.hT, [(wt("2e1")[0], ACT.Relu, 1.0, e1[:, :]), (wt("2e2")[0], ACT.Identity, 1.0, e2[:, :])], net.hT)
        w_step = sb("w_step", [P, D])
        steps = 5
        with nc.Fori(0, steps) as step:
            net.aggregate(w_step[:, :], load=[(w_step[:, :], a["L2_gnn_conv_w"].rearrange("l i o -> (l i) o")
                                               [bass.ds(step * D, D), :])])
            net.gru(wt("2ih"), wt("2hh"), [b2i[:, g:g + 1] for g in range(3)], [b2h[:, g:g + 1] for g in range(3)],
                    [b2s[:, g:g + 1] for g in range(3)])
        net.dense(net.hT, [(wt("2d1")[0], ACT.Relu, 1.0, d1[:, :]), (wt("2d2")[0], ACT.Sigmoid, 1.0, d2[:, :])], net.hT,
                  first_relu=True)

        net.norm(add=True)
        net.aggregate()
        net.dense(net.aggT, [(wt("3")[0], ACT.Identity, 1.0, b3[:, :])], net.hT)
        net.finish(out)


def kernel(**inputs):
    import concourse.bacc as bacc
    from concourse.bass_utils import run_bass_kernel_spmd

    nc = bacc.Bacc("TRN2", target_bir_lowering=False, num_devices=1)
    arrays, aps = {}, {}
    for name, value in inputs.items():
        value = np.ascontiguousarray(value)
        arrays[f"in_{name}"] = value
        aps[name] = nc.dram_tensor(f"in_{name}", value.shape, mybir.dt.from_np(value.dtype), kind="ExternalInput").ap()
    out = nc.dram_tensor("out", (N, D), F32, kind="ExternalOutput").ap()
    program(nc, aps, out)
    result = run_bass_kernel_spmd(nc, [arrays], core_ids=[0])
    return np.asarray(result.results[0]["out"])
```
